# Optimizing a Trainium2 kernel written in Bass

```python
import numpy as np
import jax
import jax.numpy as jnp

def _softmax(x, axis=-1):
    return jax.nn.softmax(x, axis=axis)

def _gelu(x):
    return jax.nn.gelu(x, approximate=True)

def _silu(x):
    return jax.nn.silu(x)

def _sigmoid(x):
    return jax.nn.sigmoid(x)

def _layernorm(x, axis=-1, eps=1e-05):
    m = jnp.mean(x, axis=axis, keepdims=True)
    v = jnp.var(x, axis=axis, keepdims=True)
    return (x - m) / jnp.sqrt(v + eps)

def _scatter_add(tgt, idx, src, axis=0):
    return tgt.at[idx].add(src)

def _segment_sum(src, seg, n):
    return jax.ops.segment_sum(src, seg, n)
kernel_name = 'mk_seq_postln_d1_jaxref_r8_bed05b'

def setup_inputs(seed: int=0):
    np.random.seed(seed)
    _w = jnp.asarray

    def _L0_attn_setup():
        import jax, jax.numpy as jnp
        import numpy as np
        N_HEADS = 16
        key = jax.random.key(seed)
        k1, k2, k3, k4 = jax.random.split(key, 4)
        B, T, C = (2, 256, 128)
        x = jax.random.normal(k1, (B, T, C), dtype=jnp.float32)
        s = 1.0 / np.sqrt(C)
        Wq = jax.random.normal(k2, (C, C), dtype=jnp.float32) * s
        Wk = jax.random.normal(k3, (C, C), dtype=jnp.float32) * s
        Wv = jax.random.normal(k4, (C, C), dtype=jnp.float32) * s
        return {'x': x, 'Wq': Wq, 'Wk': Wk, 'Wv': Wv}
    _L0_attn_in = _L0_attn_setup()

    def _L0_ffn_setup():
        import jax, jax.numpy as jnp
        import numpy as np
        DIM = 128
        DEPTH = 6
        HEADS = 16
        DIM_HEAD = 64
        WINDOW = 32
        INNER = HEADS * DIM_HEAD
        DIM_INNER = int(DIM * 4 * 2 / 3)
        QK_SCALE = 8.0

        def shift_tokens(t):
            a, s = jnp.split(t, 2, -1)
            s = jnp.pad(s, ((0, 0), (1, 0), (0, 0)))[:, :-1]
            return jnp.concatenate([a, s], -1)

        def l2norm(t):
            return t / jnp.maximum(jnp.linalg.norm(t, axis=-1, keepdims=True), 1e-12)

        def rotate_half(x):
            x1, x2 = jnp.split(x, 2, -1)
            return jnp.concatenate([-x2, x1], -1)

        def rotary_tables(n):
            half = jnp.arange(0, DIM_HEAD, 2, dtype=jnp.float32)
            inv_freq = 1.0 / 10000.0 ** (half / DIM_HEAD)
            t = jnp.arange(n, dtype=jnp.float32)
            freqs = t[:, None] * inv_freq[None, :]
            freqs = jnp.concatenate([freqs, freqs], -1)
            base_scale = (half + 0.4 * DIM_HEAD) / (1.4 * DIM_HEAD)
            power = (t - n // 2) / (WINDOW // 2)
            scale = base_scale[None, :] ** power[:, None]
            scale = jnp.concatenate([scale, scale], -1)
            return (freqs, scale)

        def local_attention(q, k, v):
            b, h, n, d = q.shape
            w = WINDOW
            nw = n // w
            bq = q.reshape(b, h, nw, w, d)
            bk = k.reshape(b, h, nw, w, d)
            bv = v.reshape(b, h, nw, w, d)

            def look(t):
                p = jnp.pad(t, ((0, 0), (0, 0), (1, 0), (0, 0), (0, 0)))
                return jnp.concatenate([p[:, :, :nw], p[:, :, 1:]], axis=3)
            bk2, bv2 = (look(bk), look(bv))
            seq = jnp.arange(n).reshape(nw, w)
            seq_p = jnp.pad(seq, ((1, 0), (0, 0)), constant_values=-1)
            jt = jnp.concatenate([seq_p[:nw], seq_p[1:]], axis=1)
            it = seq[:, :, None]
            jb = jt[:, None, :]
            mask = (it < jb) | (it > jb + w) | (jb == -1)
            sim = jnp.einsum('bhwie,bhwje->bhwij', bq, bk2) * QK_SCALE
            sim = jnp.where(mask, -jnp.finfo(sim.dtype).max, sim)
            attn = jax.nn.softmax(sim, -1)
            out = jnp.einsum('bhwij,bhwje->bhwie', attn, bv2)
            return out.reshape(b, h, n, d)

        def attn_layer(x, Wqkv, qs, ksc, Wo):
            b, n, _ = x.shape
            qkv = x @ Wqkv
            q, k, v = jnp.split(qkv, 3, -1)
            sh = lambda t: t.reshape(b, n, HEADS, DIM_HEAD).transpose(0, 2, 1, 3)
            q, k, v = (sh(q), sh(k), sh(v))
            q = l2norm(q) * qs
            k = l2norm(k) * ksc
            freqs, scale = rotary_tables(n)
            cos, sin = (jnp.cos(freqs), jnp.sin(freqs))
            q = q * cos * scale + rotate_half(q) * sin * scale
            inv = 1.0 / scale
            k = k * cos * inv + rotate_half(k) * sin * inv
            out = local_attention(q, k, v)
            out = out.transpose(0, 2, 1, 3).reshape(b, n, INNER)
            return out @ Wo

        def ffn_layer(x, g, bln, W1, b1, W2, b2):
            mu = x.mean(-1, keepdims=True)
            var = ((x - mu) ** 2).mean(-1, keepdims=True)
            xn = (x - mu) / jnp.sqrt(var + 1e-05) * g + bln
            hg = xn @ W1 + b1
            a, gate = jnp.split(hg, 2, -1)
            return a * jax.nn.gelu(gate, approximate=False) @ W2 + b2
        key = jax.random.key(seed)
        ks = jax.random.split(key, 8)
        B, N = (2, 256)
        init = lambda k, shape: jax.random.normal(k, shape, jnp.float32) * 0.02
        return {'x': jax.random.normal(ks[0], (B, N, DIM), jnp.float32), 'Wqkv': init(ks[1], (DEPTH, DIM, 3 * INNER)), 'q_scale': jnp.ones((DEPTH, DIM_HEAD), jnp.float32), 'k_scale': jnp.ones((DEPTH, DIM_HEAD), jnp.float32), 'Wo': init(ks[2], (DEPTH, INNER, DIM)), 'ln_g': jnp.ones((DEPTH, DIM), jnp.float32), 'ln_b': jnp.zeros((DEPTH, DIM), jnp.float32), 'W1': init(ks[3], (DEPTH, DIM, 2 * DIM_INNER)), 'b1': jnp.zeros((DEPTH, 2 * DIM_INNER), jnp.float32), 'W2': init(ks[4], (DEPTH, DIM_INNER, DIM)), 'b2': jnp.zeros((DEPTH, DIM), jnp.float32)}
    _L0_ffn_in = _L0_ffn_setup()
    _d = {'L0_attn_x': _L0_attn_in['x'], 'L0_attn_Wq': _L0_attn_in['Wq'], 'L0_attn_Wk': _L0_attn_in['Wk'], 'L0_attn_Wv': _L0_attn_in['Wv'], 'L0_ffn_Wqkv': _L0_ffn_in['Wqkv'], 'L0_ffn_q_scale': _L0_ffn_in['q_scale'], 'L0_ffn_k_scale': _L0_ffn_in['k_scale'], 'L0_ffn_Wo': _L0_ffn_in['Wo'], 'L0_ffn_ln_g': _L0_ffn_in['ln_g'], 'L0_ffn_ln_b': _L0_ffn_in['ln_b'], 'L0_ffn_W1': _L0_ffn_in['W1'], 'L0_ffn_b1': _L0_ffn_in['b1'], 'L0_ffn_W2': _L0_ffn_in['W2'], 'L0_ffn_b2': _L0_ffn_in['b2']}
    _x0 = _d['L0_attn_x']
    _d['L0_attn_x'] = jax.random.normal(jax.random.fold_in(jax.random.key(seed), 1), (8, 512, 128), dtype=_x0.dtype)
    del _x0
    return _d

def reference(L0_attn_x, L0_attn_Wq, L0_attn_Wk, L0_attn_Wv, L0_ffn_Wqkv, L0_ffn_q_scale, L0_ffn_k_scale, L0_ffn_Wo, L0_ffn_ln_g, L0_ffn_ln_b, L0_ffn_W1, L0_ffn_b1, L0_ffn_W2, L0_ffn_b2):

    def _L0_attn_ref(x, Wq, Wk, Wv):
        import jax, jax.numpy as jnp
        import numpy as np
        N_HEADS = 16
        B, T, C = x.shape
        H = N_HEADS
        d = C // H
        q = (x @ Wq.T).reshape(B, T, H, d)
        k = (x @ Wk.T).reshape(B, T, H, d)
        v = (x @ Wv.T).reshape(B, T, H, d)
        wei = jnp.einsum('bqhd,bkhd->bhqk', q, k) * C ** (-0.5)
        causal = jnp.tril(jnp.ones((T, T), dtype=bool))
        wei = jnp.where(causal, wei, -jnp.inf)
        wei = jax.nn.softmax(wei, axis=-1)
        out = jnp.einsum('bhqk,bkhd->bqhd', wei, v)
        return out.reshape(B, T, C)

    def _L0_ffn_ref(x, Wqkv, q_scale, k_scale, Wo, ln_g, ln_b, W1, b1, W2, b2):
        import jax, jax.numpy as jnp
        import numpy as np
        DIM = 128
        DEPTH = 6
        HEADS = 16
        DIM_HEAD = 64
        WINDOW = 32
        INNER = HEADS * DIM_HEAD
        DIM_INNER = int(DIM * 4 * 2 / 3)
        QK_SCALE = 8.0

        def shift_tokens(t):
            a, s = jnp.split(t, 2, -1)
            s = jnp.pad(s, ((0, 0), (1, 0), (0, 0)))[:, :-1]
            return jnp.concatenate([a, s], -1)

        def l2norm(t):
            return t / jnp.maximum(jnp.linalg.norm(t, axis=-1, keepdims=True), 1e-12)

        def rotate_half(x):
            x1, x2 = jnp.split(x, 2, -1)
            return jnp.concatenate([-x2, x1], -1)

        def rotary_tables(n):
            half = jnp.arange(0, DIM_HEAD, 2, dtype=jnp.float32)
            inv_freq = 1.0 / 10000.0 ** (half / DIM_HEAD)
            t = jnp.arange(n, dtype=jnp.float32)
            freqs = t[:, None] * inv_freq[None, :]
            freqs = jnp.concatenate([freqs, freqs], -1)
            base_scale = (half + 0.4 * DIM_HEAD) / (1.4 * DIM_HEAD)
            power = (t - n // 2) / (WINDOW // 2)
            scale = base_scale[None, :] ** power[:, None]
            scale = jnp.concatenate([scale, scale], -1)
            return (freqs, scale)

        def local_attention(q, k, v):
            b, h, n, d = q.shape
            w = WINDOW
            nw = n // w
            bq = q.reshape(b, h, nw, w, d)
            bk = k.reshape(b, h, nw, w, d)
            bv = v.reshape(b, h, nw, w, d)

            def look(t):
                p = jnp.pad(t, ((0, 0), (0, 0), (1, 0), (0, 0), (0, 0)))
                return jnp.concatenate([p[:, :, :nw], p[:, :, 1:]], axis=3)
            bk2, bv2 = (look(bk), look(bv))
            seq = jnp.arange(n).reshape(nw, w)
            seq_p = jnp.pad(seq, ((1, 0), (0, 0)), constant_values=-1)
            jt = jnp.concatenate([seq_p[:nw], seq_p[1:]], axis=1)
            it = seq[:, :, None]
            jb = jt[:, None, :]
            mask = (it < jb) | (it > jb + w) | (jb == -1)
            sim = jnp.einsum('bhwie,bhwje->bhwij', bq, bk2) * QK_SCALE
            sim = jnp.where(mask, -jnp.finfo(sim.dtype).max, sim)
            attn = jax.nn.softmax(sim, -1)
            out = jnp.einsum('bhwij,bhwje->bhwie', attn, bv2)
            return out.reshape(b, h, n, d)

        def attn_layer(x, Wqkv, qs, ksc, Wo):
            b, n, _ = x.shape
            qkv = x @ Wqkv
            q, k, v = jnp.split(qkv, 3, -1)
            sh = lambda t: t.reshape(b, n, HEADS, DIM_HEAD).transpose(0, 2, 1, 3)
            q, k, v = (sh(q), sh(k), sh(v))
            q = l2norm(q) * qs
            k = l2norm(k) * ksc
            freqs, scale = rotary_tables(n)
            cos, sin = (jnp.cos(freqs), jnp.sin(freqs))
            q = q * cos * scale + rotate_half(q) * sin * scale
            inv = 1.0 / scale
            k = k * cos * inv + rotate_half(k) * sin * inv
            out = local_attention(q, k, v)
            out = out.transpose(0, 2, 1, 3).reshape(b, n, INNER)
            return out @ Wo

        def ffn_layer(x, g, bln, W1, b1, W2, b2):
            mu = x.mean(-1, keepdims=True)
            var = ((x - mu) ** 2).mean(-1, keepdims=True)
            xn = (x - mu) / jnp.sqrt(var + 1e-05) * g + bln
            hg = xn @ W1 + b1
            a, gate = jnp.split(hg, 2, -1)
            return a * jax.nn.gelu(gate, approximate=False) @ W2 + b2
        for i in range(DEPTH):
            x = attn_layer(shift_tokens(x), Wqkv[i], q_scale[i], k_scale[i], Wo[i]) + x
            x = ffn_layer(shift_tokens(x), ln_g[i], ln_b[i], W1[i], b1[i], W2[i], b2[i]) + x
        return x
    x = L0_attn_x
    x = _layernorm(x + _L0_attn_ref(x, L0_attn_Wq, L0_attn_Wk, L0_attn_Wv), axis=-1)
    x = _layernorm(x + _L0_ffn_ref(x, L0_ffn_Wqkv, L0_ffn_q_scale, L0_ffn_k_scale, L0_ffn_Wo, L0_ffn_ln_g, L0_ffn_ln_b, L0_ffn_W1, L0_ffn_b1, L0_ffn_W2, L0_ffn_b2), axis=-1)
    return x

_drawn_inputs = setup_inputs


def setup_inputs(seed=0):
    import zlib

    import numpy as np

    out = dict(_drawn_inputs(seed))
    spreads = {'L0_ffn_q_scale': (1.0, 0.6),
     'L0_ffn_k_scale': (1.0, 0.6),
     'L0_ffn_ln_g': (1.0, 0.6),
     'L0_ffn_ln_b': (0.0, 0.8),
     'L0_ffn_b1': (0.0, 0.8),
     'L0_ffn_b2': (0.0, 0.1)}
    factors = {'L0_ffn_W1': 3.672, 'L0_ffn_W2': 3.609}
    for name, (base, spread) in spreads.items():
        noise = np.random.default_rng([zlib.crc32(name.encode()), seed]).standard_normal(out[name].shape)
        drawn = base * np.exp(spread * noise) if base else spread * noise
        out[name] = jnp.asarray(drawn.astype(out[name].dtype))
    for name, factor in factors.items():
        out[name] = (out[name] * factor).astype(out[name].dtype)
    return out
```

```python
from contextlib import ExitStack

import concourse.bass as bass
import numpy as np
from concourse import mybir

ALU = mybir.AluOpType
ACT = mybir.ActivationFunctionType
AX = mybir.AxisListType
F32 = mybir.dt.float32
F16 = mybir.dt.float16
BF16 = mybir.dt.bfloat16

P = 128
B, T, C = 8, 512, 128
NT = T // P
H1 = 16
D1 = C // H1
SLOT = 32
G1 = H1 * SLOT // P
SCALE1 = float(C) ** -0.5
PAIRS1 = H1 // 2
STEPS1 = PAIRS1 * NT
DEPTH = 6
H, D, WIN = 16, 64, 32
INNER = H * D
QK_SCALE = 8.0
HH = H // 2
HP = HH // 2
NW = P // WIN
UNITS = NT * 2
ITERS = DEPTH * B
FF = C * 4 * 2 // 3
FCH = [min(P, FF - c * P) for c in range(-(-FF // P))]
NF = len(FCH)
PAD = WIN
COLS = PAD + T + 4
EPS = 1e-5
NEG = -1e30


def constants():
    f = np.float32
    half = np.arange(0, D, 2, dtype=f)
    inv_freq = f(1.0) / f(10000.0) ** (half / f(D))
    t = np.arange(T, dtype=f)
    freqs = t[:, None] * inv_freq[None, :]
    base = (half + f(0.4 * D)) / f(1.4 * D)
    power = (t - T // 2) / f(WIN // 2)
    scale = base[None, :] ** power[:, None]
    cos, sin = np.cos(freqs), np.sin(freqs)
    rows = np.zeros((T, 2, 2, D), f)
    for i, s in enumerate((scale * f(QK_SCALE), f(1.0) / scale)):
        rows[:, 0, i, :] = np.concatenate([cos * s, cos * s], -1)
        rows[:, 1, i, :] = np.concatenate([sin * s, -sin * s], -1)
    rot = rows.reshape(NT, P, 4 * D).transpose(1, 0, 2).reshape(P, NT * 4 * D)
    q = np.arange(P)[:, None] % WIN + WIN
    k = np.arange(2 * WIN)[None, :]
    mask = np.where((q < k) | (q > k + WIN), f(NEG), f(0.0))
    first = mask.copy()
    first[:WIN, :WIN] = NEG
    causal = np.where(np.arange(P)[:, None] < np.arange(P)[None, :], f(NEG), f(0.0))
    row = np.arange(P)[:, None] % SLOT // D1
    parts = np.where(np.concatenate([row == 1, row == 2], 1), f(-1.0), f(0.0))
    return {
        "rot": np.ascontiguousarray(rot.astype(f)),
        "masks": np.ascontiguousarray(np.concatenate([mask, first, causal], 1).astype(f)),
        "ident": np.eye(P, dtype=f),
        "parts": np.ascontiguousarray(parts),
    }


def need(eng, sem, value):
    if isinstance(value, int) and value <= 0:
        return
    eng.wait_ge(sem, value)


def build(nc, x, wq1_d, wk1_d, wv1_d, wqkv_d, qs_d, ks_d, wo_d, lng_d, lnb_d, w1_d, b1_d, w2_d, b2_d,
          rot_d, masks_d, ident_d, parts_d, out):
    with ExitStack() as ctx:
        def sb(name, shape, dt=F32):
            return ctx.enter_context(nc.sbuf_tensor(name, shape, dt))

        def sem(name):
            return ctx.enter_context(nc.semaphore(name))

        stream = sb("stream", [P, B * COLS])
        x1 = sb("x1", [P, B * NT, C])
        ident = sb("ident", [P, P])
        identb = sb("identb", [P, P], BF16)
        masks = sb("masks", [P, 4 * WIN + P])
        maskb = sb("maskb", [P, 4 * WIN + P], BF16)
        ones = sb("ones", [P, P])
        mean_w = sb("mean_w", [P, P])
        neghalf = sb("neghalf", [P, H])
        parts = sb("parts", [P, 2])
        w1nat = sb("w1nat", [P, 3, C])
        wq1 = sb("wq1", [P, H1, SLOT])
        wk1 = sb("wk1", [P, H1, SLOT])
        wv1 = sb("wv1", [P, C])
        xin = sb("xin", [P, NT, C])
        x1t = sb("x1t", [P, T])
        qk1 = sb("qk1", [P, 2, G1, T], F16)
        v1 = sb("v1", [P, NT, C])
        p1 = sb("p1", [P, 2, 2, T])
        pt1 = sb("pt1", [P, 2, T])
        mx1 = sb("mx1", [P, 2])
        nb1 = sb("nb1", [P, 2, 2])
        l1 = sb("l1", [P, NT, H1])
        rl1 = sb("rl1", [P, NT, H1])
        y1 = sb("y1", [P, NT, C])
        bn = sb("bn", [P, NT, 6])
        mv = sb("mv", [P, NT, 2])
        vv1 = sb("vv1", [P, NT])
        rs1 = sb("rs1", [P, NT])
        wqkv = sb("wqkv", [P, 3 * INNER])
        wo = sb("wo", [P, INNER // P, C])
        w1 = sb("w1", [P, 2 * FF])
        w2 = sb("w2", [P, NF, C])
        qks = sb("qks", [P, 2 * D])
        rot = sb("rot", [P, NT * 2, 2 * D])
        tab = sb("tab", [P, NT * 2, 2 * D])
        lng = sb("lng", [P, DEPTH])
        lnb = sb("lnb", [P, DEPTH])
        b1a = sb("b1a", [P, NF, DEPTH])
        b1g = sb("b1g", [P, NF, DEPTH])
        b2 = sb("b2", [P, DEPTH])
        xs = sb("xs", [P, PAD + T])
        sq = sb("sq", [P, 2 * HH, D])
        ss = sb("ss", [P, 2 * HH])
        cl = sb("cl", [P, 2 * HH])
        rn = sb("rn", [P, 2 * HH])
        qkn = sb("qkn", [P, 2 * HH, D])
        qkc = sb("qkc", [P, 2 * HH, D])
        qks_ = sb("qksin", [P, 2 * HH, D])
        qkr = sb("qkr", [P, 2 * HH, D])
        qT = sb("qT", [P, HP, P])
        kT = sb("kT", [P, 2 * HP, PAD + T])
        vwin = sb("vwin", [P, 4, NW, HP * D])
        mx = sb("mx", [P, HH])
        sm = sb("sm", [P, HH, 2 * WIN])
        pr = sb("pr", [P, 2, HH, 2 * WIN])
        lsum = sb("lsum", [P, HH])
        rl = sb("rl", [P, HH])
        pT = sb("pT", [P, HP, P])
        on = sb("on", [P, HH, D])
        oT = sb("oT", [P, 2, 2 * HP, P])
        fd = sb("fd", [P, T])
        fsq = sb("fsq", [P, T])
        fv = sb("fv", [P, NT])
        frs = sb("frs", [P, NT])
        fdg = sb("fdg", [P, NT, P])
        fxn = sb("fxn", [P, T])
        fxa = sb("fxa", [P, T])
        fg = sb("fg", [P, NF, T])
        fh = sb("fh", [P, NF, T])

        banks = ctx.enter_context(nc.psum_tensor("banks", [P, 8, 512], F32))
        QK, VB, TR, SB_, PO, OB, FB = banks[:, 0:2, :], banks[:, 2, :], banks[:, 3, :], banks[:, 4, :], \
            banks[:, 5, :], banks[:, 6, :], banks[:, 7, :]

        consts_in, params_in, w1nat_in, xin_in = sem("consts_in"), sem("params_in"), sem("w1nat_in"), sem("xin_in")
        wqkv_in, wo_in, w1_in, w2_in, qks_in = sem("wqkv_in"), sem("wo_in"), sem("w1_in"), sem("w2_in"), sem("qks_in")
        zeroed, bf_ready = sem("zeroed"), sem("bf_ready")
        wt_done, wt_copied = sem("wt_done"), sem("wt_copied")
        xt1_done, xt1_copied = sem("xt1_done"), sem("xt1_copied")
        pj1_done, hi1_done, lo1_done = sem("pj1_done"), sem("hi1_done"), sem("lo1_done")
        v1_done, v1_copied = sem("v1_done"), sem("v1_copied")
        s1_done, mx1_done, nb1_done, exp1_done = sem("s1_done"), sem("mx1_done"), sem("nb1_done"), sem("exp1_done")
        pt1_done, pt1a_copied, pt1b_copied, pv1_done = sem("pt1_done"), sem("pt1a_copied"), sem("pt1b_copied"), sem("pv1_done")
        ln1_chain, rl1_done, stats1_done, rs1_done = sem("ln1_chain"), sem("rl1_done"), sem("stats1_done"), sem("rs1_done")
        back1_done, stream_in = sem("back1_done"), sem("stream_in")
        xs_done, proj_done, v_done, sq_done, v_copied = sem("xs_done"), sem("proj_done"), sem("v_done"), sem("sq_done"), sem("v_copied")
        red_done, clamp_done, rn_done, norm_qk, cos_done, sin_done, rot_done, tab_done = (
            sem("red_done"), sem("clamp_done"), sem("rn_done"), sem("norm_qk"), sem("cos_done"), sem("sin_done"), sem("rot_done"), sem("tab_done"))
        kt_done, qt_done, kt_copied, qt_copied = sem("kt_done"), sem("qt_done"), sem("kt_copied"), sem("qt_copied")
        s_even, pv_odd = sem("s_even"), sem("pv_odd")
        s_done, max_done, sub_done, exp_done = sem("s_done"), sem("max_done"), sem("sub_done"), sem("exp_done")
        pt_done, pt_copied, pv_done, sum_done, rl_done, o_done = (
            sem("pt_done"), sem("pt_copied"), sem("pv_done"), sem("sum_done"), sem("rl_done"), sem("o_done"))
        ot_done, ot_copied, y_done, y_added = sem("ot_done"), sem("ot_copied"), sem("y_done"), sem("y_added")
        mean_done, dev_done, fsq_done, var_done, fv_done, frs_done, dg_done, bc_done, xn_done, xa_done = (
            sem("mean_done"), sem("dev_done"), sem("fsq_done"), sem("var_done"), sem("fv_done"), sem("frs_done"),
            sem("dg_done"), sem("bc_done"), sem("xn_done"), sem("xa_done"))
        gate_done, gelu_done, up_done, h_done, down_done, ff_added = (
            sem("gate_done"), sem("gelu_done"), sem("up_done"), sem("h_done"), sem("down_done"), sem("ff_added"))
        flat_done, back_done, fin_sum, fin_stats, fin_aggr, fin_var, fin_rs, fin_done, stored = (
            sem("flat_done"), sem("back_done"), sem("fin_sum"), sem("fin_stats"), sem("fin_aggr"), sem("fin_var"), sem("fin_rs"), sem("fin_done"), sem("stored"))

        N_CONST = 4

        def plain(eng):
            eng.wait_ge(consts_in, 16 * N_CONST)

        def batch(b, lo, n):
            return bass.ds(b * COLS + lo, n)

        def heads1(step):
            return step // NT, step % NT

        block = ctx.enter_context(nc.Block())

        @block.sync
        def _(sp):
            sp.dma_start(ident[:], ident_d).then_inc(consts_in, 16)
            sp.dma_start(masks[:], masks_d).then_inc(consts_in, 16)
            sp.dma_start(parts[:], parts_d).then_inc(consts_in, 16)
            for i, w in enumerate((wq1_d, wk1_d, wv1_d)):
                sp.dma_start(w1nat[:, i, :], w).then_inc(w1nat_in, 16)
            sp.dma_start(rot[:].rearrange("p a b -> p (a b)"), rot_d).then_inc(consts_in, 16)

            def load_qkv(l):
                sp.dma_start(wqkv[:], wqkv_d[bass.ds(l, 1)].rearrange("a p n -> p (a n)")).then_inc(wqkv_in, 16)

            def load_scales(l):
                sp.dma_start(qks[:, 0:D], qs_d[bass.ds(l, 1), :].broadcast_to([P, D])).then_inc(qks_in, 16)
                sp.dma_start(qks[:, D:2 * D], ks_d[bass.ds(l, 1), :].broadcast_to([P, D])).then_inc(qks_in, 16)

            def load_out(l):
                sp.dma_start(wo[:], wo_d[bass.ds(l, 1)].rearrange("a (t p) n -> p (a t) n", p=P)).then_inc(wo_in, 16)

            def load_ff(l):
                sp.dma_start(w1[:], w1_d[bass.ds(l, 1)].rearrange("a p n -> p (a n)")).then_inc(w1_in, 16)
                for c in range(NF):
                    sp.dma_start(w2[0:FCH[c], c, :],
                                 w2_d[bass.ds(l, 1), c * P:c * P + FCH[c], :].rearrange("a p n -> p (a n)")
                                 ).then_inc(w2_in, 16)

            def load_x(b):
                sp.dma_start(xin[:], x[bass.ds(b, 1)].rearrange("a (t p) c -> p (a t) c", p=P)).then_inc(xin_in, 16)

            load_x(0)
            load_qkv(0)
            load_scales(0)
            load_out(0)
            load_ff(0)
            for l in range(DEPTH):
                sp.dma_start(lng[:, l:l + 1], lng_d[l, :].rearrange("(p a) -> p a", a=1)).then_inc(params_in, 16)
                sp.dma_start(lnb[:, l:l + 1], lnb_d[l, :].rearrange("(p a) -> p a", a=1)).then_inc(params_in, 16)
                sp.dma_start(b2[:, l:l + 1], b2_d[l, :].rearrange("(p a) -> p a", a=1)).then_inc(params_in, 16)
                for c in range(NF):
                    for dst, at in ((b1a, 0), (b1g, FF)):
                        sp.dma_start(dst[0:FCH[c], c, l:l + 1],
                                     b1_d[l, at + c * P:at + c * P + FCH[c]].rearrange("(p a) -> p a", a=1)
                                     ).then_inc(params_in, 16)
            with sp.Fori(1, B) as b:
                sp.wait_ge(ln1_chain, b * 6 - 4)
                load_x(b)
            with sp.Fori(1, DEPTH) as l:
                sp.wait_ge(v_done, l * (2 * UNITS * B))
                load_qkv(l)
                sp.wait_ge(tab_done, l * B)
                load_scales(l)
                sp.wait_ge(y_done, l * (NT * B))
                load_out(l)
                sp.wait_ge(down_done, l * B)
                load_ff(l)
            with sp.Fori(0, B) as b:
                sp.wait_ge(fin_done, b + 1)
                sp.dma_start(out[bass.ds(b, 1)].rearrange("a (t p) c -> p (a t) c", p=P), y1[:]).then_inc(stored, 16)
            sp.wait_ge(stored, B * 16)

        @block.gpsimd
        def _(pool):
            pool.memset(stream[:], 0.0).then_inc(zeroed, 1)
            pool.memset(kT[:, :, 0:PAD], 0.0).then_inc(zeroed, 1)
            pool.memset(ones[:], 1.0).then_inc(zeroed, 1)
            pool.memset(mean_w[:], 1.0 / C).then_inc(zeroed, 1)
            pool.memset(neghalf[:], -0.5).then_inc(zeroed, 1)
            pool.memset(wq1[:], 0.0).then_inc(zeroed, 1)
            pool.memset(wk1[:], 0.0).then_inc(zeroed, 1)
            with pool.Fori(0, B) as b:
                pool.wait_ge(ln1_chain, b * 6 + 4)
                pool.tensor_tensor(rs1[:], vv1[:], neghalf[:, 0:NT], ALU.pow).then_inc(rs1_done, 1)

            def step(it, u, tail=False):
                n = it * UNITS + u
                first = isinstance(it, int) and it == 0
                if not (first and u < 1) and not (tail and u > 0):
                    need(pool, norm_qk, n)
                    need(pool, rot_done, n - 1)
                    need(pool, tab_done, (it + 1) if u else it)
                    pool.tensor_tensor(qks_[:].rearrange("p (a h) d -> p a h d", a=2),
                                       qkn[:].rearrange("p (a h) d -> p a h d", a=2),
                                       tab[:, 2 * ((u - 1) % UNITS // 2) + 1, :].rearrange("p (a o d) -> p a o d", a=2, o=1)
                                       .broadcast_to([P, 2, HH, D]),
                                       ALU.mult).then_inc(sin_done, 1)
                if tail:
                    return
                if u == 0:
                    pool.wait_ge(qks_in, (it // B) * 32 + 32)
                    pool.wait_ge(consts_in, 16 * N_CONST)
                    need(pool, cos_done, n)
                    need(pool, sin_done, n)
                    pool.tensor_tensor(tab[:], rot[:], qks[:].unsqueeze(1).broadcast_to([P, NT * 2, 2 * D]),
                                       ALU.mult).then_inc(tab_done, 1)
                if u == 4 and not first:
                    ff_rstd(it)
                pool.wait_ge(clamp_done, n + 1)
                need(pool, norm_qk, n)
                pool.tensor_tensor(rn[:], cl[:], neghalf[:], ALU.pow).then_inc(rn_done, 1)

            def ff_rstd(it):
                pool.wait_ge(fv_done, it)
                pool.tensor_tensor(frs[:], fv[:], neghalf[:, 0:NT], ALU.pow).then_inc(frs_done, 1)

            for u in range(UNITS):
                step(0, u)
            with pool.Fori(1, ITERS) as it:
                for u in range(UNITS):
                    step(it, u)
            step(ITERS, 0, tail=True)
            ff_rstd(ITERS)
            with pool.Fori(0, B) as b:
                pool.wait_ge(fin_var, b + 1)
                pool.tensor_tensor(rs1[:], vv1[:], neghalf[:, 0:NT], ALU.pow).then_inc(fin_rs, 1)

        @block.scalar
        def _(act):
            act.wait_ge(consts_in, 16 * N_CONST)
            nc.scalar.activation(identb[:], ident[:], ACT.Copy).then_inc(bf_ready, 1)
            nc.scalar.activation(maskb[:], masks[:], ACT.Copy).then_inc(bf_ready, 1)
            act.wait_ge(wt_done, 1)
            act.wait_ge(zeroed, 7)
            for i, w in enumerate((wq1, wk1)):
                for r in range(3):
                    nc.scalar.activation(w[:, :, r * D1:(r + 1) * D1],
                                         FB[:, i * C:(i + 1) * C].rearrange("p (h d) -> p h d", d=D1),
                                         ACT.Copy).then_inc(wt_copied, 1)
            nc.scalar.activation(wv1[:], FB[:, 2 * C:3 * C], ACT.Copy).then_inc(wt_copied, 1)
            def attend(b):
                act.wait_ge(xt1_done, b + 1)
                nc.scalar.activation(x1t[:], FB, ACT.Copy).then_inc(xt1_copied, 1)
                for m in range(2 * G1):
                    i, g = m % 2, m // 2
                    act.wait_ge(pj1_done, b * (2 * G1) + m + 1)
                    nc.scalar.activation(qk1[:, i, g, :], banks[:, m % 4, :], ACT.Copy).then_inc(hi1_done, 1)
                act.wait_ge(v1_done, b + 1)
                nc.scalar.activation(v1[:].rearrange("p t c -> p (t c)"), FB, ACT.Copy).then_inc(v1_copied, 1)

                def exps(s):
                    n = b * STEPS1 + s
                    hp, i = heads1(s)
                    act.wait_ge(nb1_done, n + 1)
                    if s == 0:
                        need(act, pt1_done, b * (2 * STEPS1))
                    if s >= 2:
                        act.wait_ge(pt1_done, 2 * n - 2)
                    for r in range(2):
                        h = 2 * hp + r
                        nc.scalar.activation(p1[:, s % 2, r, 0:(i + 1) * P], banks[:, 2 * (s % 2) + r, 0:(i + 1) * P],
                                             ACT.Exp, bias=nb1[:, s % 2, r:r + 1], scale=SCALE1,
                                             accum_out=l1[:, i, h:h + 1]).then_inc(exp1_done, 1)

                def turned(s):
                    n = b * STEPS1 + s
                    hp, i = heads1(s)
                    act.wait_ge(pt1_done, 2 * n + 2)
                    need(act, pv1_done, n)
                    nc.scalar.activation(pt1[:, 1, 0:(i + 1) * P], banks[:, 5, 0:(i + 1) * P],
                                         ACT.Copy).then_inc(pt1b_copied, 1)

                for s in range(STEPS1):
                    exps(s)
                    if s >= 1:
                        turned(s - 1)
                turned(STEPS1 - 1)
                act.wait_ge(back1_done, b + 1)
                nc.scalar.activation(stream[0:64, batch(b, PAD, T)], FB[0:64, :], ACT.Copy).then_inc(stream_in, 1)
                nc.scalar.activation(stream[64:128, batch(b, PAD + 1, T)], FB[64:128, :], ACT.Copy).then_inc(stream_in, 1)

            attend(0)
            with act.Fori(1, B) as b:
                attend(b)

            act.wait_ge(params_in, 16 * DEPTH * (3 + 2 * NF))

            def step(it, u, tail=False):
                n = it * UNITS + u
                first = isinstance(it, int) and it == 0
                def values(v2):
                    act.wait_ge(v_done, 2 * n + v2 + 1)
                    need(act, pv_done, n - 3)
                    nc.scalar.activation(vwin[:, u % 4, 2 * v2:2 * v2 + 2, :].rearrange("p w n -> p (w n)"), VB,
                                         ACT.Copy).then_inc(v_copied, 1)

                if not tail:
                    values(0)
                if not (first and u < 2) and not (tail and u > 1):
                    act.wait_ge(sub_done, n - 1)
                    need(act, pt_done, n - 3)
                    need(act, sum_done, n - 3)
                    nc.scalar.activation(pr[:, u % 2], sm[:], ACT.Exp).then_inc(exp_done, 1)
                if not tail:
                    act.wait_ge(proj_done, n + 1)
                    need(act, red_done, n)
                    nc.scalar.activation(sq[:].rearrange("p h d -> p (h d)"), QK.rearrange("p a n -> p (a n)"),
                                         ACT.Square).then_inc(sq_done, 1)

                if not (first and u < 2) and not (tail and u > 1):
                    act.wait_ge(pt_done, n - 1)
                    need(act, pv_done, n - 2)
                    nc.scalar.activation(pT[:].rearrange("p h t -> p (h t)"), PO, ACT.Copy).then_inc(pt_copied, 1)
                if not tail:
                    values(1)
                if not first and not tail:
                    ff(it, u, 0)
                if not (first and u < 3):
                    m = (u - 3) % UNITS
                    tile = ((n - 3) // 2) if isinstance(n, int) else (it * NT + (u - 3) // 2)
                    act.wait_ge(ot_done, n - 2)
                    need(act, y_done, tile - 1)
                    nc.scalar.activation(oT[:, m // 2 % 2, m % 2 * HP:(m % 2 + 1) * HP, :].rearrange("p h t -> p (h t)"),
                                         PO, ACT.Copy).then_inc(ot_copied, 1)
                if not (first and u < 1) and not (tail and u > 0):
                    pj, ph = (u - 1) % UNITS // 2, (u - 1) % 2
                    act.wait_ge(kt_done, n)
                    need(act, s_done, n - 1)
                    nc.scalar.activation(kT[:, ph * HP:(ph + 1) * HP, PAD + pj * P:PAD + (pj + 1) * P],
                                         TR.rearrange("p (h t) -> p h t", t=P), ACT.Copy).then_inc(kt_copied, 1)
                    act.wait_ge(qt_done, n)
                    nc.scalar.activation(qT[:].rearrange("p h t -> p (h t)"), TR, ACT.Copy).then_inc(qt_copied, 1)
                if not first and not tail:
                    ff(it, u, 1)
                    ff(it, u, 2)

            def ff(it, u, spot):
                l = (it - 1) // B
                if (u, spot) == (3, 1):
                    act.wait_ge(dev_done, it)
                    nc.scalar.activation(fsq[:], fd[:], ACT.Square).then_inc(fsq_done, 1)
                if (u, spot) == (4, 2):
                    act.wait_ge(xn_done, it)
                    nc.scalar.activation(fxa[:], fxn[:], ACT.Identity, scale=lng[:, bass.ds(l, 1)],
                                         bias=lnb[:, bass.ds(l, 1)]).then_inc(xa_done, 1)
                if u == 5:
                    c = spot
                    m = FCH[c]
                    act.wait_ge(gate_done, (it - 1) * NF + c + 1)
                    nc.scalar.activation(fg[0:m, c, :], FB[0:m, :], ACT.Gelu,
                                         bias=b1g[0:m, c, bass.ds(l, 1)]).then_inc(gelu_done, 1)

            for u in range(UNITS):
                step(0, u)
            with act.Fori(1, ITERS) as it:
                for u in range(UNITS):
                    step(it, u)
            for u in range(3):
                step(ITERS, u, tail=True)
            for u in range(3, UNITS):
                for spot in range(3):
                    ff(ITERS, u, spot)
            def finish(b):
                act.wait_ge(ff_added, 2 * ITERS)
                need(act, back_done, b)
                nc.scalar.activation(fd[0:64, :], stream[0:64, batch(b, PAD, T)], ACT.Copy).then_inc(flat_done, 1)
                nc.scalar.activation(fd[64:128, :], stream[64:128, batch(b, PAD + 1, T)], ACT.Copy).then_inc(flat_done, 1)

            finish(0)
            with act.Fori(1, B) as b:
                finish(b)

        @block.vector
        def _(dve):
            dve.wait_ge(consts_in, 16 * N_CONST)
            def attend(b):
                for m in range(2 * G1):
                    i, g = m % 2, m // 2
                    dve.wait_ge(hi1_done, b * (2 * G1) + m + 1)
                    nc.vector.scalar_tensor_tensor(out=qk1[:, i, g, :], in0=qk1[:, i, g, :], scalar=parts[:, i:i + 1],
                                                   in1=banks[:, m % 4, :], op0=ALU.mult, op1=ALU.add).then_inc(lo1_done, 1)

                def maxima(s):
                    n = b * STEPS1 + s
                    hp, i = heads1(s)
                    dve.wait_ge(s1_done, n + 1)
                    need(dve, nb1_done, n)
                    nc.vector.tensor_reduce(mx1[:], banks[:, 2 * (s % 2):2 * (s % 2) + 2, 0:(i + 1) * P], AX.X,
                                            ALU.max).then_inc(mx1_done, 1)
                    dve.wait_ge(mx1_done, n + 1)
                    if s >= 2:
                        dve.wait_ge(exp1_done, 2 * n - 2)
                    nc.vector.tensor_scalar(nb1[:, s % 2, :], mx1[:], -SCALE1, None, ALU.mult).then_inc(nb1_done, 1)

                def turned(s):
                    n = b * STEPS1 + s
                    hp, i = heads1(s)
                    dve.wait_ge(pt1_done, 2 * n + 1)
                    need(dve, pv1_done, n)
                    nc.vector.tensor_copy(pt1[:, 0, 0:(i + 1) * P], banks[:, 4, 0:(i + 1) * P]).then_inc(pt1a_copied, 1)

                for s in range(STEPS1):
                    maxima(s)
                    if s >= 1:
                        turned(s - 1)
                turned(STEPS1 - 1)
                base = b * 6
                dve.wait_ge(exp1_done, (b + 1) * (2 * STEPS1))
                nc.vector.reciprocal(rl1[:], l1[:]).then_inc(rl1_done, 1)
                dve.wait_ge(rl1_done, b + 1)
                dve.wait_ge(pv1_done, (b + 1) * STEPS1)
                need(dve, back1_done, b)
                nc.vector.tensor_tensor(y1[:].rearrange("p t (h d) -> p (t h) d", d=D1),
                                        banks[:, 6, :].rearrange("p (h d) -> p h d", d=D1),
                                        rl1[:].rearrange("p t h -> p (t h)").unsqueeze(2).broadcast_to([P, NT * H1, D1]),
                                        ALU.mult).then_inc(ln1_chain, 1)
                dve.wait_ge(ln1_chain, base + 1)
                nc.vector.tensor_tensor(y1[:], y1[:], xin[:], ALU.add).then_inc(ln1_chain, 1)
                dve.wait_ge(ln1_chain, base + 2)
                for t in range(NT):
                    last = nc.vector.bn_stats(bn[:, t, :], y1[:, t, :])
                last.then_inc(stats1_done, 1)
                plain(dve)
                dve.wait_ge(stats1_done, b + 1)
                for t in range(NT):
                    last = nc.vector.bn_aggr(mv[:, t, :], bn[:, t, :])
                last.then_inc(ln1_chain, 1)
                dve.wait_ge(ln1_chain, base + 3)
                nc.vector.tensor_scalar(vv1[:], mv[:, :, 1], EPS, None, ALU.add).then_inc(ln1_chain, 1)
                dve.wait_ge(rs1_done, b + 1)
                for t in range(NT):
                    last = nc.vector.tensor_scalar(y1[:, t, :], y1[:, t, :], mv[:, t, 0:1], rs1[:, t:t + 1],
                                                   ALU.subtract, ALU.mult)
                last.then_inc(ln1_chain, 1)
                dve.wait_ge(ln1_chain, base + 5)
                nc.vector.tensor_copy(x1[:, bass.ds(b * NT, NT), :], y1[:]).then_inc(ln1_chain, 1)

            attend(0)
            with dve.Fori(1, B) as b:
                attend(b)

            dve.wait_ge(stream_in, 2 * B)
            dve.wait_ge(zeroed, 7)
            dve.wait_ge(params_in, 16 * DEPTH * (3 + 2 * NF))

            def step(it, u, tail=False):
                n = it * UNITS + u
                first = isinstance(it, int) and it == 0
                if u == 0 and not tail:
                    plain(dve)
                    need(dve, v_done, 2 * n)
                    nc.vector.tensor_copy(xs[:], stream[:, batch(it % B, 0, PAD + T)]).then_inc(xs_done, 1)
                if not (first and u < 2) and not (tail and u > 1):
                    dve.wait_ge(s_done, n - 1)
                    nc.vector.tensor_reduce(mx[:], SB_.rearrange("p (h k) -> p h k", k=2 * WIN), AX.X,
                                            ALU.max).then_inc(max_done, 1)
                    dve.wait_ge(max_done, n - 1)
                    need(dve, exp_done, n - 2)
                    nc.vector.tensor_tensor(sm[:], SB_.rearrange("p (h k) -> p h k", k=2 * WIN),
                                            mx[:].unsqueeze(2).broadcast_to([P, HH, 2 * WIN]),
                                            ALU.subtract).then_inc(sub_done, 1)
                if not (first and u < 1) and not (tail and u > 0):
                    dve.wait_ge(norm_qk, n)
                    need(dve, tab_done, (it + 1) if u else it)
                    nc.vector.tensor_tensor(qkc[:].rearrange("p (a h) d -> p a h d", a=2),
                                            qkn[:].rearrange("p (a h) d -> p a h d", a=2),
                                            tab[:, 2 * ((u - 1) % UNITS // 2), :].rearrange("p (a o d) -> p a o d", a=2, o=1)
                                            .broadcast_to([P, 2, HH, D]),
                                            ALU.mult).then_inc(cos_done, 1)
                if not (first and u < 1) and not (tail and u > 0):
                    dve.wait_ge(cos_done, n)
                    dve.wait_ge(sin_done, n)
                    need(dve, qt_done, n - 1)
                    nc.vector.tensor_tensor(qkr[:].rearrange("p h (t f) -> p h t f", t=2),
                                            qkc[:].rearrange("p h (t f) -> p h t f", t=2),
                                            qks_[:].rearrange("p h (t f) -> p h t f", t=2)[:, :, ::-1, :],
                                            ALU.add).then_inc(rot_done, 1)
                if not tail:
                    dve.wait_ge(sq_done, n + 1)
                    nc.vector.tensor_reduce(ss[:], sq[:], AX.X, ALU.add).then_inc(red_done, 1)
                    dve.wait_ge(red_done, n + 1)
                    need(dve, rn_done, n)
                    nc.vector.tensor_scalar(cl[:], ss[:], 1e-24, None, ALU.max).then_inc(clamp_done, 1)
                if not first and not tail:
                    ff(it, u, 0)
                if not (first and u < 2) and not (tail and u > 1):
                    dve.wait_ge(exp_done, n - 1)
                    nc.vector.tensor_reduce(lsum[:], pr[:, u % 2], AX.X, ALU.add).then_inc(sum_done, 1)
                    dve.wait_ge(sum_done, n - 1)
                    nc.vector.reciprocal(rl[:], lsum[:]).then_inc(rl_done, 1)
                    dve.wait_ge(rl_done, n - 1)
                    dve.wait_ge(pv_done, n - 1)
                    need(dve, ot_done, n - 2)
                    nc.vector.tensor_tensor(on[:], OB.rearrange("p (h d) -> p h d", d=D),
                                            rl[:].unsqueeze(2).broadcast_to([P, HH, D]), ALU.mult).then_inc(o_done, 1)
                if not first and not tail:
                    ff(it, u, 1)
                if not tail:
                    dve.wait_ge(rn_done, n + 1)
                    dve.wait_ge(proj_done, n + 1)
                    need(dve, sin_done, n)
                    need(dve, cos_done, n)
                    nc.vector.tensor_tensor(qkn[:], QK.rearrange("p a (h d) -> p (a h) d", d=D),
                                            rn[:].unsqueeze(2).broadcast_to([P, 2 * HH, D]), ALU.mult).then_inc(norm_qk, 1)
                if (u - 3) % 2 == 1 and not (first and u < 4):
                    tile = it * NT + (u - 4) // 2 + 1
                    bb = (it if u >= 3 else it - 1) % B
                    at = PAD + (u - 4) % UNITS // 2 * P
                    dve.wait_ge(y_done, tile)
                    lo, hi = stream[0:64, batch(bb, at, P)], stream[64:128, batch(bb, at + 1, P)]
                    nc.vector.tensor_tensor(lo, VB[0:64, 0:P], lo, ALU.add).then_inc(y_added, 1)
                    nc.vector.tensor_tensor(hi, VB[64:128, 0:P], hi, ALU.add).then_inc(y_added, 1)
                if not first and not tail:
                    ff(it, u, 2)

            def ff(it, u, spot):
                bb, l = (it - 1) % B, (it - 1) // B
                if (u, spot) == (3, 0):
                    dve.wait_ge(mean_done, it)
                    dve.wait_ge(y_added, it * (2 * NT))
                    nc.vector.tensor_tensor(fd[:], stream[:, batch(bb, PAD, T)], FB, ALU.subtract).then_inc(dev_done, 1)
                if (u, spot) == (3, 2):
                    dve.wait_ge(var_done, it)
                    nc.vector.tensor_scalar(fv[:], FB[:, 0:NT], EPS, None, ALU.add).then_inc(fv_done, 1)
                if (u, spot) == (4, 0):
                    dve.wait_ge(frs_done, it)
                    nc.vector.tensor_tensor(fdg[:], ident[:].unsqueeze(1).broadcast_to([P, NT, P]),
                                            frs[:].unsqueeze(2).broadcast_to([P, NT, P]), ALU.mult).then_inc(dg_done, 1)
                if (u, spot) == (4, 2):
                    dve.wait_ge(bc_done, it)
                    nc.vector.tensor_tensor(fxn[:], fd[:], FB, ALU.mult).then_inc(xn_done, 1)
                if u == 6:
                    c = spot
                    m = FCH[c]
                    dve.wait_ge(up_done, (it - 1) * NF + c + 1)
                    dve.wait_ge(gelu_done, (it - 1) * NF + c + 1)
                    nc.vector.scalar_tensor_tensor(out=fh[0:m, c, :], in0=FB[0:m, :], scalar=b1a[0:m, c, bass.ds(l, 1)],
                                                   in1=fg[0:m, c, :], op0=ALU.add, op1=ALU.mult).then_inc(h_done, 1)
                if (u, spot) == (7, 0):
                    dve.wait_ge(down_done, it)
                    lo, hi = stream[0:64, batch(bb, PAD, T)], stream[64:128, batch(bb, PAD + 1, T)]
                    nc.vector.scalar_tensor_tensor(out=lo, in0=FB[0:64, :], scalar=b2[0:64, bass.ds(l, 1)], in1=lo,
                                                   op0=ALU.add, op1=ALU.add).then_inc(ff_added, 1)
                    nc.vector.scalar_tensor_tensor(out=hi, in0=FB[64:128, :], scalar=b2[64:128, bass.ds(l, 1)], in1=hi,
                                                   op0=ALU.add, op1=ALU.add).then_inc(ff_added, 1)

            for u in range(UNITS):
                step(0, u)
            with dve.Fori(1, ITERS) as it:
                for u in range(UNITS):
                    step(it, u)
            for u in range(3):
                step(ITERS, u, tail=True)
            for u in range(3, UNITS):
                for spot in range(3):
                    ff(ITERS, u, spot)
            def finish(b):
                dve.wait_ge(back_done, b + 1)
                need(dve, stored, b * 16)
                nc.vector.tensor_tensor(y1[:], FB.rearrange("p (t c) -> p t c", c=C), x1[:, bass.ds(b * NT, NT), :],
                                        ALU.add).then_inc(fin_sum, 1)
                dve.wait_ge(fin_sum, b + 1)
                for t in range(NT):
                    last = nc.vector.bn_stats(bn[:, t, :], y1[:, t, :])
                last.then_inc(fin_stats, 1)
                plain(dve)
                dve.wait_ge(fin_stats, b + 1)
                for t in range(NT):
                    last = nc.vector.bn_aggr(mv[:, t, :], bn[:, t, :])
                last.then_inc(fin_aggr, 1)
                dve.wait_ge(fin_aggr, b + 1)
                nc.vector.tensor_scalar(vv1[:], mv[:, :, 1], EPS, None, ALU.add).then_inc(fin_var, 1)
                dve.wait_ge(fin_rs, b + 1)
                for t in range(NT):
                    last = nc.vector.tensor_scalar(y1[:, t, :], y1[:, t, :], mv[:, t, 0:1], rs1[:, t:t + 1],
                                                   ALU.subtract, ALU.mult)
                last.then_inc(fin_done, 1)

            finish(0)
            with dve.Fori(1, B) as b:
                finish(b)

        @block.tensor
        def _(pe):
            def turn(dst, src):
                return nc.tensor.transpose(dst, src, ident[:])

            pe.wait_ge(consts_in, 16 * N_CONST)
            pe.wait_ge(w1nat_in, 48)
            for i in range(3):
                last = turn(FB[:, i * C:(i + 1) * C], w1nat[:, i, :])
            last.then_inc(wt_done, 1)
            pe.wait_ge(wt_copied, 7)
            pe.wait_ge(bf_ready, 2)
            def attend(b):
                pe.wait_ge(xin_in, b * 16 + 16)
                need(pe, stream_in, b * 2)
                for t in range(NT):
                    last = turn(FB[:, t * P:(t + 1) * P], xin[:, t, :])
                last.then_inc(xt1_done, 1)
                pe.wait_ge(xt1_copied, b + 1)
                for m in range(2 * G1):
                    i, g = m % 2, m // 2
                    if m < 4:
                        need(pe, exp1_done, b * (2 * STEPS1))
                    else:
                        pe.wait_ge(lo1_done, b * (2 * G1) + m - 3)
                    w = (wq1, wk1)[i]
                    nc.tensor.matmul(banks[:, m % 4, :], w[:, g * (P // SLOT):(g + 1) * (P // SLOT), :].rearrange("p h s -> p (h s)"),
                                     x1t[:], start=True, stop=True).then_inc(pj1_done, 1)
                for t in range(NT):
                    last = nc.tensor.matmul(FB[:, t * C:(t + 1) * C], x1t[:, t * P:(t + 1) * P], wv1[:], start=True, stop=True)
                last.then_inc(v1_done, 1)
                pe.wait_ge(lo1_done, (b + 1) * (2 * G1))

                def scores(s):
                    n = b * STEPS1 + s
                    hp, i = heads1(s)
                    if s >= 2:
                        pe.wait_ge(exp1_done, 2 * n - 2)
                    for r in range(2):
                        h = 2 * hp + r
                        g, at = h // (P // SLOT), h % (P // SLOT) * SLOT
                        bank = banks[:, 2 * (s % 2) + r, :]
                        nc.tensor.matmul(bank[:, 0:(i + 1) * P], qk1[at:at + SLOT, 0, g, i * P:(i + 1) * P],
                                         qk1[at:at + SLOT, 1, g, 0:(i + 1) * P], start=True, stop=False,
                                         tile_position=(at, 0))
                        last = nc.tensor.matmul(bank[:, i * P:(i + 1) * P], identb[:], maskb[:, 4 * WIN:4 * WIN + P],
                                                start=False, stop=True)
                    last.then_inc(s1_done, 1)

                def values(s):
                    n = b * STEPS1 + s
                    hp, i = heads1(s)
                    for r in range(2):
                        pe.wait_ge(exp1_done, 2 * n + r + 1)
                        need(pe, (pt1a_copied, pt1b_copied)[r], n)
                        for k in range(i + 1):
                            last = turn(banks[:, 4 + r, k * P:(k + 1) * P], p1[:, s % 2, r, k * P:(k + 1) * P])
                        last.then_inc(pt1_done, 1)
                    for r in range(2):
                        h = 2 * hp + r
                        pe.wait_ge((pt1a_copied, pt1b_copied)[r], n + 1)
                        for k in range(i + 1):
                            last = nc.tensor.matmul(banks[:, 6, i * C + h * D1:i * C + (h + 1) * D1], pt1[:, r, k * P:(k + 1) * P],
                                                    v1[:, k, h * D1:(h + 1) * D1], start=(k == 0), stop=(k == i))
                    last.then_inc(pv1_done, 1)

                scores(0)
                pe.wait_ge(v1_copied, b + 1)
                for s in range(STEPS1):
                    if s + 1 < STEPS1:
                        scores(s + 1)
                    if s == 0:
                        need(pe, ln1_chain, b * 6)
                    values(s)
                pe.wait_ge(ln1_chain, b * 6 + 5)
                for t in range(NT):
                    last = turn(FB[:, t * P:(t + 1) * P], y1[:, t, :])
                last.then_inc(back1_done, 1)

            attend(0)
            with pe.Fori(1, B) as b:
                attend(b)

            pe.wait_ge(stream_in, 2 * B)

            def step(it, u, tail=False):
                n = it * UNITS + u
                first = isinstance(it, int) and it == 0
                j, hf = u // 2, u % 2
                pj, ph = (u - 1) % UNITS // 2, (u - 1) % 2
                with_s = not (first and u < 1) and not (tail and u > 0)
                with_o = not (first and u < 2) and not (tail and u > 1)
                with_t = not (first and u < 3)
                wv = wqkv[:, 2 * INNER + hf * 512:2 * INNER + (hf + 1) * 512].rearrange("p (h r d) -> p r h d", r=2, d=D)

                def values(v2):
                    need(pe, v_copied, 2 * n + v2)
                    if v2 == 0:
                        cnt = ((n - 3) // 2) if isinstance(n, int) else it * NT + (u - 3) // 2
                        need(pe, y_added, 2 * cnt)
                    for w in range(2 * v2, 2 * v2 + 2):
                        for r in range(2):
                            at = j * P + w * WIN
                            last = nc.tensor.matmul(VB[64 * r:64 * r + 64, (w % 2) * 256:(w % 2 + 1) * 256].rearrange("p (h d) -> p h d", d=D),
                                                    xs[:, at:at + 2 * WIN], wv[:, r], start=True, stop=True,
                                                    tile_position=(0, 64 * r))
                    last.then_inc(v_done, 1)

                def scores(par):
                    r = 64 * par
                    for h in range(par, HH, 2):
                        for w in range(NW):
                            at = pj * P + w * WIN
                            last = nc.tensor.matmul(SB_[32 * w:32 * w + 32, h * 2 * WIN:(h + 1) * 2 * WIN],
                                                    qT[r:r + 64, h // 2, 32 * w:32 * w + 32],
                                                    kT[r:r + 64, ph * HP + h // 2, at:at + 2 * WIN],
                                                    start=False, stop=True, tile_position=(r, 32 * w),
                                                    skip_group_check=True)
                    return last

                def results(par):
                    r = 64 * par
                    for h in range(par, HH, 2):
                        for w in range(NW):
                            last = nc.tensor.matmul(OB[32 * w:32 * w + 32, h * D:(h + 1) * D],
                                                    pT[r:r + 64, h // 2, 32 * w:32 * w + 32],
                                                    vwin[r:r + 64, (u - 2) % 4, w, h // 2 * D:(h // 2 + 1) * D],
                                                    start=True, stop=True, tile_position=(r, 32 * w))
                    return last

                if not tail:
                    if u == 0:
                        pe.wait_ge(wqkv_in, (it // B) * 16 + 16)
                        pe.wait_ge(xs_done, it + 1)
                    values(0)
                    need(pe, norm_qk, n)
                    need(pe, sq_done, n)
                    for i in range(2):
                        last = nc.tensor.matmul(QK[:, i, :], xs[:, PAD + j * P:PAD + (j + 1) * P],
                                                wqkv[:, i * INNER + hf * 512:i * INNER + hf * 512 + 512], start=True, stop=True)
                    last.then_inc(proj_done, 1)
                if with_o:
                    pe.wait_ge(exp_done, n - 1)
                    pe.wait_ge(v_copied, 2 * (n - 1))
                    need(pe, ot_copied, n - 3)
                    for h in range(HP):
                        last = turn(PO[:, h * P:(h + 1) * P], pr[:, u % 2, 2 * h:2 * h + 2, :].rearrange("p h d -> p (h d)"))
                    last.then_inc(pt_done, 1)
                if not tail:
                    values(1)
                if not first and not tail:
                    ff(it, u, 0)
                if with_t:
                    pe.wait_ge(o_done, n - 2)
                    if tail:
                        pe.wait_ge(ot_copied, n - 3)
                        pe.wait_ge(pt_copied, min(n - 1, ITERS * UNITS))
                    else:
                        pe.wait_ge(pt_copied, n - 1)
                    for h in range(HP):
                        last = turn(PO[:, h * P:(h + 1) * P], on[:, 2 * h:2 * h + 2, :].rearrange("p h d -> p (h d)"))
                    last.then_inc(ot_done, 1)
                if with_o:
                    plain(pe)
                    pe.wait_ge(pt_copied, n - 1)
                    need(pe, o_done, n - 2)
                    results(1).then_inc(pv_odd, 1)
                if with_s:
                    pe.wait_ge(rot_done, n)
                    need(pe, qt_copied, n - 1)
                    for h in range(HP):
                        last = turn(TR[:, h * P:(h + 1) * P], qkr[:, HH + 2 * h:HH + 2 * h + 2, :].rearrange("p h d -> p (h d)"))
                    last.then_inc(kt_done, 1)
                if with_o:
                    plain(pe)
                    pe.wait_ge(pv_odd, n - 1)
                    results(0).then_inc(pv_done, 1)
                if not first and not tail:
                    ff(it, u, 1)
                if with_s:
                    pe.wait_ge(kt_copied, n)
                    for h in range(HP):
                        last = turn(TR[:, h * P:(h + 1) * P], qkr[:, 2 * h:2 * h + 2, :].rearrange("p h d -> p (h d)"))
                    last.then_inc(qt_done, 1)
                    need(pe, sub_done, n - 1)
                    m = maskb[:, 0:2 * WIN] if pj else maskb[:, 2 * WIN:4 * WIN]
                    nc.tensor.matmul(SB_.rearrange("p (h k) -> p h k", k=2 * WIN), identb[:],
                                     m.unsqueeze(1).broadcast_to([P, HH, 2 * WIN]), start=True, stop=False,
                                     skip_group_check=True)
                if (u - 3) % 2 == 1 and not (first and u < 4):
                    if u == 4 and not tail:
                        pe.wait_ge(wo_in, (it // B) * 16 + 16)
                    pe.wait_ge(ot_copied, n - 2)
                    need(pe, v_copied, 2 * n + 2 if not tail else 2 * ITERS * UNITS)
                    t = (u - 4) % UNITS // 2 % 2
                    for h in range(2 * HP):
                        last = nc.tensor.matmul(VB[:, 0:P], wo[:, h, :], oT[:, t, h, :], start=(h == 0), stop=(h == 2 * HP - 1))
                    last.then_inc(y_done, 1)
                if with_s:
                    plain(pe)
                    pe.wait_ge(qt_copied, n)
                    scores(0).then_inc(s_even, 1)
                if not first and not tail:
                    ff(it, u, 2)
                if with_s:
                    plain(pe)
                    pe.wait_ge(s_even, n)
                    scores(1).then_inc(s_done, 1)

            def ff(it, u, spot):
                bb, l = (it - 1) % B, (it - 1) // B
                if (u, spot) == (3, 0):
                    pe.wait_ge(y_added, it * (2 * NT))
                    nc.tensor.matmul(FB, mean_w[:], stream[:, batch(bb, PAD, T)], start=True, stop=True).then_inc(mean_done, 1)
                if (u, spot) == (3, 2):
                    pe.wait_ge(fsq_done, it)
                    for t in range(NT):
                        last = nc.tensor.matmul(FB[:, t:t + 1], fsq[:, t * P:(t + 1) * P], mean_w[:, 0:1], start=True, stop=True)
                    last.then_inc(var_done, 1)
                if (u, spot) == (4, 1):
                    pe.wait_ge(dg_done, it)
                    nc.tensor.matmul(FB, ones[:], fdg[:].rearrange("p t c -> p (t c)"), start=True, stop=True).then_inc(bc_done, 1)
                if u == 5:
                    c = spot
                    m = FCH[c]
                    if c == 0:
                        pe.wait_ge(w1_in, l * 16 + 16)
                        pe.wait_ge(xa_done, it)
                    else:
                        pe.wait_ge(gelu_done, (it - 1) * NF + c)
                    nc.tensor.matmul(FB[0:m, :], w1[:, FF + c * P:FF + c * P + m], fxa[:], start=True, stop=True).then_inc(gate_done, 1)
                if u == 6:
                    c = spot
                    m = FCH[c]
                    if c == 0:
                        pe.wait_ge(gelu_done, it * NF)
                    else:
                        pe.wait_ge(h_done, (it - 1) * NF + c)
                    nc.tensor.matmul(FB[0:m, :], w1[:, c * P:c * P + m], fxa[:], start=True, stop=True).then_inc(up_done, 1)
                if (u, spot) == (7, 0):
                    pe.wait_ge(h_done, it * NF)
                    pe.wait_ge(w2_in, l * (16 * NF) + 16 * NF)
                    for c in range(NF):
                        m = FCH[c]
                        last = nc.tensor.matmul(FB, w2[0:m, c, :], fh[0:m, c, :], start=(c == 0), stop=(c == NF - 1))
                    last.then_inc(down_done, 1)

            for u in range(UNITS):
                step(0, u)
            with pe.Fori(1, ITERS) as it:
                for u in range(UNITS):
                    step(it, u)
            for u in range(3):
                step(ITERS, u, tail=True)
            for u in range(3, UNITS):
                for spot in range(3):
                    ff(ITERS, u, spot)
            def finish(b):
                pe.wait_ge(flat_done, b * 2 + 2)
                need(pe, fin_sum, b)
                for t in range(NT):
                    last = turn(FB[:, t * P:(t + 1) * P], fd[:, t * P:(t + 1) * P])
                last.then_inc(back_done, 1)

            finish(0)
            with pe.Fori(1, B) as b:
                finish(b)


_INS = ['L0_attn_x', 'L0_attn_Wq', 'L0_attn_Wk', 'L0_attn_Wv', 'L0_ffn_Wqkv', 'L0_ffn_q_scale', 'L0_ffn_k_scale',
        'L0_ffn_Wo', 'L0_ffn_ln_g', 'L0_ffn_ln_b', 'L0_ffn_W1', 'L0_ffn_b1', 'L0_ffn_W2', 'L0_ffn_b2']
_CONSTS = ['rot', 'masks', 'ident', 'parts']


def kernel(**inputs):
    import numpy as _np
    import concourse.bacc as _bacc
    from concourse import mybir as _mybir
    from concourse.bass_utils import run_bass_kernel_spmd as _run

    nc = _bacc.Bacc("TRN2", target_bir_lowering=False, num_devices=1)
    arrays, args = {}, []
    consts = constants()
    for name in _INS + _CONSTS:
        a = _np.ascontiguousarray(inputs[name] if name in _INS else consts[name])
        arrays[f"in_{name}_dram"] = a
        args.append(nc.dram_tensor(f"in_{name}_dram", a.shape, _mybir.dt.from_np(a.dtype), kind="ExternalInput").ap())
    args.append(nc.dram_tensor("out_0_dram", (B, T, C), _mybir.dt.float32, kind="ExternalOutput").ap())
    build(nc, *args)
    r = _run(nc, [arrays], core_ids=[0])
    return r.results[0]["out_0_dram"]
```

```python
from contextlib import ExitStack

import concourse.bass as bass
import numpy as np
from concourse import mybir

ALU = mybir.AluOpType
ACT = mybir.ActivationFunctionType
AX = mybir.AxisListType
F32 = mybir.dt.float32
F16 = mybir.dt.float16
BF16 = mybir.dt.bfloat16

P = 128
B, T, C = 8, 512, 128
NT = T // P
H1 = 16
D1 = C // H1
SLOT = 32
G1 = H1 * SLOT // P
SCALE1 = float(C) ** -0.5
GH = P // SLOT
MAXROW = 3 * D1
MAXES = 2 * NT
QUADS = G1 * NT
DEPTH = 6
H, D, WIN = 16, 64, 32
INNER = H * D
QK_SCALE = 8.0
HH = H // 2
HP = HH // 2
NW = P // WIN
UNITS = NT * 2
ITERS = DEPTH * B
FF = C * 4 * 2 // 3
FCH = [min(P, FF - c * P) for c in range(-(-FF // P))]
NF = len(FCH)
PAD = WIN
COLS = PAD + T + 4
EPS = 1e-5
NEG = -1e30


def constants():
    f = np.float32
    half = np.arange(0, D, 2, dtype=f)
    inv_freq = f(1.0) / f(10000.0) ** (half / f(D))
    t = np.arange(T, dtype=f)
    freqs = t[:, None] * inv_freq[None, :]
    base = (half + f(0.4 * D)) / f(1.4 * D)
    power = (t - T // 2) / f(WIN // 2)
    scale = base[None, :] ** power[:, None]
    cos, sin = np.cos(freqs), np.sin(freqs)
    rows = np.zeros((T, 2, 2, D), f)
    for i, s in enumerate((scale * f(QK_SCALE), f(1.0) / scale)):
        rows[:, 0, i, :] = np.concatenate([cos * s, cos * s], -1)
        rows[:, 1, i, :] = np.concatenate([sin * s, -sin * s], -1)
    rot = rows.reshape(NT, P, 4 * D).transpose(1, 0, 2).reshape(P, NT * 4 * D)
    q = np.arange(P)[:, None] % WIN + WIN
    k = np.arange(2 * WIN)[None, :]
    mask = np.where((q < k) | (q > k + WIN), f(NEG), f(0.0))
    first = mask.copy()
    first[:WIN, :WIN] = NEG
    causal = np.where(np.arange(P)[:, None] < np.arange(P)[None, :], f(NEG), f(0.0))
    row = np.arange(P)[:, None] % SLOT // D1
    at_max = np.arange(P)[:, None] % SLOT == MAXROW
    parts = np.concatenate([-(row == 1).astype(f), at_max.astype(f) - (row == 2), at_max.astype(f)], 1).astype(f)
    return {
        "rot": np.ascontiguousarray(rot.astype(f)),
        "masks": np.ascontiguousarray(np.concatenate([mask, first, causal, causal.T], 1).astype(f)),
        "ident": np.eye(P, dtype=f),
        "parts": np.ascontiguousarray(parts),
    }


def need(eng, sem, value):
    if isinstance(value, int) and value <= 0:
        return
    eng.wait_ge(sem, value)


def build(nc, x, wq1_d, wk1_d, wv1_d, wqkv_d, qs_d, ks_d, wo_d, lng_d, lnb_d, w1_d, b1_d, w2_d, b2_d,
          rot_d, masks_d, ident_d, parts_d, out):
    with ExitStack() as ctx:
        def sb(name, shape, dt=F32):
            return ctx.enter_context(nc.sbuf_tensor(name, shape, dt))

        def sem(name):
            return ctx.enter_context(nc.semaphore(name))

        stream = sb("stream", [P, B * COLS])
        x1 = sb("x1", [P, B * NT, C])
        ident = sb("ident", [P, P])
        identb = sb("identb", [P, P], BF16)
        identh = sb("identh", [P, P], F16)
        masks = sb("masks", [P, 4 * WIN + 2 * P])
        maskb = sb("maskb", [P, 4 * WIN + 2 * P], BF16)
        ones = sb("ones", [P, P])
        mean_w = sb("mean_w", [P, P])
        neghalf = sb("neghalf", [P, H])
        parts = sb("parts", [P, 3])
        w1nat = sb("w1nat", [P, 3, C])
        wq1 = sb("wq1", [P, H1, SLOT])
        wk1 = sb("wk1", [P, H1, SLOT])
        wv1 = sb("wv1", [P, C])
        xin = sb("xin", [P, NT, C])
        x1t = sb("x1t", [P, T])
        qk1 = sb("qk1", [P, 2, G1, T], F16)
        v1 = sb("v1", [P, NT, H1, SLOT])
        mx1 = sb("mx1", [P, NT, H1])
        mnat = sb("mnat", [P, NT, H1, SLOT], F16)
        qm1 = sb("qm1", [P, 2, T], F16)
        p1_vwin = sb("p1_vwin", [P, 2 * GH * T])
        p1 = p1_vwin[:].rearrange("p (a r t) -> p a r t", a=2, r=GH)
        ot1 = sb("ot1", [P, T])
        rl1 = sb("rl1", [P, NT * GH])
        y1 = sb("y1", [P, NT, C])
        bn = sb("bn", [P, NT, 6])
        mv = sb("mv", [P, NT, 2])
        vv1 = sb("vv1", [P, NT])
        rs1 = sb("rs1", [P, NT])
        wqkv = sb("wqkv", [P, 3 * INNER])
        wo = sb("wo", [P, INNER // P, C])
        w1 = sb("w1", [P, 2 * FF])
        w2 = sb("w2", [P, NF, C])
        qks = sb("qks", [P, 2 * D])
        rot = sb("rot", [P, NT * 2, 2 * D])
        tab = sb("tab", [P, NT * 2, 2 * D])
        lng = sb("lng", [P, DEPTH])
        lnb = sb("lnb", [P, DEPTH])
        b1a = sb("b1a", [P, NF, DEPTH])
        b1g = sb("b1g", [P, NF, DEPTH])
        b2 = sb("b2", [P, DEPTH])
        xs = sb("xs", [P, PAD + T])
        sq = sb("sq", [P, 2 * HH, D])
        ss = sb("ss", [P, 2 * HH])
        cl = sb("cl", [P, 2 * HH])
        rn = sb("rn", [P, 2 * HH])
        qkn = sb("qkn", [P, 2 * HH, D])
        qkc = sb("qkc", [P, 2 * HH, D])
        qks_ = sb("qksin", [P, 2 * HH, D])
        qkr = sb("qkr", [P, 2 * HH, D])
        qT = sb("qT", [P, HP, P])
        kT = sb("kT", [P, 2 * HP, PAD + T])
        vwin = p1_vwin[:].rearrange("p (a w n) -> p a w n", a=4, w=NW)
        mx = sb("mx", [P, HH])
        sm = sb("sm", [P, HH, 2 * WIN])
        pr = sb("pr", [P, 2, HH, 2 * WIN])
        lsum = sb("lsum", [P, HH])
        rl = sb("rl", [P, HH])
        pT = sb("pT", [P, HP, P])
        on = sb("on", [P, HH, D])
        oT = sb("oT", [P, 2, HP, P])
        fd = sb("fd", [P, T])
        fsq = sb("fsq", [P, T])
        fv = sb("fv", [P, NT])
        frs = sb("frs", [P, NT])
        fdg = sb("fdg", [P, NT, P])
        fxn = sb("fxn", [P, T])
        fxa = sb("fxa", [P, T])
        fg = sb("fg", [P, NF, T])
        fh = sb("fh", [P, NF, T])

        banks = ctx.enter_context(nc.psum_tensor("banks", [P, 8, 512], F32))
        QK, VB, TR, SB_, PO, OB, FB = banks[:, 0:2, :], banks[:, 2, :], banks[:, 3, :], banks[:, 4, :], \
            banks[:, 5, :], banks[:, 6, :], banks[:, 7, :]

        consts_in, params_in, w1nat_in, xin_in = sem("consts_in"), sem("params_in"), sem("w1nat_in"), sem("xin_in")
        wqkv_in, wo_in, w1_in, w2_in, qks_in = sem("wqkv_in"), sem("wo_in"), sem("w1_in"), sem("w2_in"), sem("qks_in")
        zeroed, bf_ready = sem("zeroed"), sem("bf_ready")
        wt_done, wt_copied = sem("wt_done"), sem("wt_copied")
        xt1_done, xt1_copied = sem("xt1_done"), sem("xt1_copied")
        pj1_done, hi1_done, lo1_done = sem("pj1_done"), sem("hi1_done"), sem("lo1_done")
        v1_done, v1_copied = sem("v1_done"), sem("v1_copied")
        s1_done, mx1_done, neg1_done, mt1_done, qm1_done = (
            sem("s1_done"), sem("mx1_done"), sem("neg1_done"), sem("mt1_done"), sem("qm1_done"))
        st1_done, exp1_done, pv1_done, ot1_copied, on1_done, rl1_done, part1_done = (
            sem("st1_done"), sem("exp1_done"), sem("pv1_done"), sem("ot1_copied"), sem("on1_done"), sem("rl1_done"),
            sem("part1_done"))
        ln1_chain, stats1_done, rs1_done = sem("ln1_chain"), sem("stats1_done"), sem("rs1_done")
        back1_done, stream_in = sem("back1_done"), sem("stream_in")
        xs_done, proj_done, v_done, sq_done, v_copied = sem("xs_done"), sem("proj_done"), sem("v_done"), sem("sq_done"), sem("v_copied")
        red_done, clamp_done, rn_done, norm_qk, cos_done, sin_done, rot_done, tab_done = (
            sem("red_done"), sem("clamp_done"), sem("rn_done"), sem("norm_qk"), sem("cos_done"), sem("sin_done"), sem("rot_done"), sem("tab_done"))
        kt_done, qt_done, kt_copied, qt_copied = sem("kt_done"), sem("qt_done"), sem("kt_copied"), sem("qt_copied")
        s_even, pv_odd = sem("s_even"), sem("pv_odd")
        s_done, max_done, sub_done, exp_done = sem("s_done"), sem("max_done"), sem("sub_done"), sem("exp_done")
        pt_done, pt_copied, pv_done, sum_done, rl_done, o_done = (
            sem("pt_done"), sem("pt_copied"), sem("pv_done"), sem("sum_done"), sem("rl_done"), sem("o_done"))
        ot_done, ot_copied, y_done, y_added = sem("ot_done"), sem("ot_copied"), sem("y_done"), sem("y_added")
        mean_done, dev_done, fsq_done, var_done, fv_done, frs_done, dg_done, bc_done, xn_done, xa_done = (
            sem("mean_done"), sem("dev_done"), sem("fsq_done"), sem("var_done"), sem("fv_done"), sem("frs_done"),
            sem("dg_done"), sem("bc_done"), sem("xn_done"), sem("xa_done"))
        gate_done, gelu_done, up_done, h_done, down_done, ff_added = (
            sem("gate_done"), sem("gelu_done"), sem("up_done"), sem("h_done"), sem("down_done"), sem("ff_added"))
        flat_done, back_done, fin_sum, fin_stats, fin_aggr, fin_var, fin_rs, fin_done, stored = (
            sem("flat_done"), sem("back_done"), sem("fin_sum"), sem("fin_stats"), sem("fin_aggr"), sem("fin_var"), sem("fin_rs"), sem("fin_done"), sem("stored"))

        N_CONST = 4

        def plain(eng):
            eng.wait_ge(consts_in, 16 * N_CONST)

        def batch(b, lo, n):
            return bass.ds(b * COLS + lo, n)

        block = ctx.enter_context(nc.Block())

        @block.sync
        def _(sp):
            sp.dma_start(ident[:], ident_d).then_inc(consts_in, 16)
            sp.dma_start(masks[:], masks_d).then_inc(consts_in, 16)
            sp.dma_start(parts[:], parts_d).then_inc(consts_in, 16)
            for i, w in enumerate((wq1_d, wk1_d, wv1_d)):
                sp.dma_start(w1nat[:, i, :], w).then_inc(w1nat_in, 16)
            sp.dma_start(rot[:].rearrange("p a b -> p (a b)"), rot_d).then_inc(consts_in, 16)

            def load_qkv(l):
                sp.dma_start(wqkv[:], wqkv_d[bass.ds(l, 1)].rearrange("a p n -> p (a n)")).then_inc(wqkv_in, 16)

            def load_scales(l):
                sp.dma_start(qks[:, 0:D], qs_d[bass.ds(l, 1), :].broadcast_to([P, D])).then_inc(qks_in, 16)
                sp.dma_start(qks[:, D:2 * D], ks_d[bass.ds(l, 1), :].broadcast_to([P, D])).then_inc(qks_in, 16)

            def load_out(l):
                sp.dma_start(wo[:], wo_d[bass.ds(l, 1)].rearrange("a (t p) n -> p (a t) n", p=P)).then_inc(wo_in, 16)

            def load_ff(l):
                sp.dma_start(w1[:], w1_d[bass.ds(l, 1)].rearrange("a p n -> p (a n)")).then_inc(w1_in, 16)
                for c in range(NF):
                    sp.dma_start(w2[0:FCH[c], c, :],
                                 w2_d[bass.ds(l, 1), c * P:c * P + FCH[c], :].rearrange("a p n -> p (a n)")
                                 ).then_inc(w2_in, 16)

            def load_x(b):
                sp.dma_start(xin[:], x[bass.ds(b, 1)].rearrange("a (t p) c -> p (a t) c", p=P)).then_inc(xin_in, 16)

            load_x(0)
            load_qkv(0)
            load_scales(0)
            load_out(0)
            load_ff(0)
            for l in range(DEPTH):
                sp.dma_start(lng[:, l:l + 1], lng_d[l, :].rearrange("(p a) -> p a", a=1)).then_inc(params_in, 16)
                sp.dma_start(lnb[:, l:l + 1], lnb_d[l, :].rearrange("(p a) -> p a", a=1)).then_inc(params_in, 16)
                sp.dma_start(b2[:, l:l + 1], b2_d[l, :].rearrange("(p a) -> p a", a=1)).then_inc(params_in, 16)
                for c in range(NF):
                    for dst, at in ((b1a, 0), (b1g, FF)):
                        sp.dma_start(dst[0:FCH[c], c, l:l + 1],
                                     b1_d[l, at + c * P:at + c * P + FCH[c]].rearrange("(p a) -> p a", a=1)
                                     ).then_inc(params_in, 16)
            with sp.Fori(1, B) as b:
                sp.wait_ge(ln1_chain, b * 5 - 4)
                load_x(b)
            with sp.Fori(1, DEPTH) as l:
                sp.wait_ge(v_done, l * (2 * UNITS * B))
                load_qkv(l)
                sp.wait_ge(tab_done, l * B)
                load_scales(l)
                sp.wait_ge(y_done, l * (UNITS * B))
                load_out(l)
                sp.wait_ge(down_done, l * B)
                load_ff(l)
            with sp.Fori(0, B) as b:
                sp.wait_ge(fin_done, b + 1)
                sp.dma_start(out[bass.ds(b, 1)].rearrange("a (t p) c -> p (a t) c", p=P), y1[:]).then_inc(stored, 16)
            sp.wait_ge(stored, B * 16)

        @block.gpsimd
        def _(pool):
            pool.memset(stream[:], 0.0).then_inc(zeroed, 1)
            pool.memset(kT[:, :, 0:PAD], 0.0).then_inc(zeroed, 1)
            pool.memset(ones[:], 1.0).then_inc(zeroed, 1)
            pool.memset(mean_w[:], 1.0 / C).then_inc(zeroed, 1)
            pool.memset(neghalf[:], -0.5).then_inc(zeroed, 1)
            pool.memset(wq1[:], 0.0).then_inc(zeroed, 1)
            pool.memset(wk1[:], 0.0).then_inc(zeroed, 1)
            pool.memset(v1[:], 0.0).then_inc(zeroed, 1)
            pool.memset(mnat[:], 0.0).then_inc(zeroed, 1)
            pool.wait_ge(zeroed, 9)
            pool.memset(v1[:, :, :, D1:D1 + 1], 1.0).then_inc(zeroed, 1)
            with pool.Fori(0, B) as b:
                pool.wait_ge(ln1_chain, b * 5 + 3)
                pool.tensor_tensor(rs1[:], vv1[:], neghalf[:, 0:NT], ALU.pow).then_inc(rs1_done, 1)

            def step(it, u):
                n = it * UNITS + u
                first = isinstance(it, int) and it == 0
                if u == 0:
                    pool.wait_ge(qks_in, (it // B) * 32 + 32)
                    pool.wait_ge(consts_in, 16 * N_CONST)
                    need(pool, cos_done, n)
                    need(pool, sin_done, n)
                    pool.tensor_tensor(tab[:], rot[:], qks[:].unsqueeze(1).broadcast_to([P, NT * 2, 2 * D]),
                                       ALU.mult).then_inc(tab_done, 1)
                if u == 4 and not first:
                    ff_rstd(it)
                pool.wait_ge(clamp_done, n + 1)
                need(pool, norm_qk, n)
                pool.tensor_tensor(rn[:], cl[:], neghalf[:], ALU.pow).then_inc(rn_done, 1)
                pool.wait_ge(norm_qk, n + 1)
                need(pool, rot_done, n)
                pool.wait_ge(tab_done, it + 1)
                pool.tensor_tensor(qks_[:].rearrange("p (a h) d -> p a h d", a=2),
                                   qkn[:].rearrange("p (a h) d -> p a h d", a=2),
                                   tab[:, 2 * (u // 2) + 1, :].rearrange("p (a o d) -> p a o d", a=2, o=1)
                                   .broadcast_to([P, 2, HH, D]),
                                   ALU.mult).then_inc(sin_done, 1)

            def ff_rstd(it):
                pool.wait_ge(fv_done, it)
                pool.tensor_tensor(frs[:], fv[:], neghalf[:, 0:NT], ALU.pow).then_inc(frs_done, 1)

            for u in range(UNITS):
                step(0, u)
            with pool.Fori(1, ITERS) as it:
                for u in range(UNITS):
                    step(it, u)
            ff_rstd(ITERS)
            with pool.Fori(0, B) as b:
                pool.wait_ge(fin_var, b + 1)
                pool.tensor_tensor(rs1[:], vv1[:], neghalf[:, 0:NT], ALU.pow).then_inc(fin_rs, 1)

        @block.scalar
        def _(act):
            act.wait_ge(consts_in, 16 * N_CONST)
            nc.scalar.activation(identb[:], ident[:], ACT.Copy).then_inc(bf_ready, 1)
            nc.scalar.activation(maskb[:], masks[:], ACT.Copy).then_inc(bf_ready, 1)
            nc.scalar.activation(identh[:], ident[:], ACT.Copy).then_inc(bf_ready, 1)
            act.wait_ge(wt_done, 1)
            act.wait_ge(zeroed, 10)
            for i, w in enumerate((wq1, wk1)):
                for r in range(3):
                    nc.scalar.activation(w[:, :, r * D1:(r + 1) * D1],
                                         FB[:, i * C:(i + 1) * C].rearrange("p (h d) -> p h d", d=D1),
                                         ACT.Copy).then_inc(wt_copied, 1)
            nc.scalar.activation(wv1[:], FB[:, 2 * C:3 * C], ACT.Copy).then_inc(wt_copied, 1)
            def attend(b):
                act.wait_ge(xt1_done, b + 1)
                nc.scalar.activation(x1t[:], FB, ACT.Copy).then_inc(xt1_copied, 1)
                for m in range(2 * G1):
                    i, g = m % 2, m // 2
                    act.wait_ge(pj1_done, b * (2 * G1) + m + 1)
                    if i:
                        nc.scalar.activation(qk1[:, 1, g, :], banks[:, m % 4, :], ACT.Identity,
                                             bias=parts[:, 2:3]).then_inc(hi1_done, 1)
                    else:
                        nc.scalar.activation(qk1[:, 0, g, :], banks[:, m % 4, :], ACT.Copy).then_inc(hi1_done, 1)
                act.wait_ge(v1_done, b + 1)
                nc.scalar.activation(v1[:, :, :, 0:D1], FB.rearrange("p (t h d) -> p t h d", h=H1, d=D1),
                                     ACT.Copy).then_inc(v1_copied, 1)

                def copy_results(g):
                    act.wait_ge(pv1_done, b * QUADS + (g + 1) * NT)
                    need(act, on1_done, b * G1 + g)
                    nc.scalar.activation(ot1[:], banks[:, 6, :], ACT.Copy).then_inc(ot1_copied, 1)

                for q in range(QUADS):
                    g, k = q // NT, q % NT
                    n = b * QUADS + q
                    for r in range(GH):
                        act.wait_ge(st1_done, n * GH + r + 1)
                        if r == 0:
                            need(act, pv1_done, n - 1)
                        nc.scalar.activation(p1[:, q % 2, r, 0:T - k * P], banks[:, 4 + r % 2, 0:T - k * P], ACT.Exp,
                                             scale=SCALE1).then_inc(exp1_done, 1)
                    if g and k == 0:
                        copy_results(g - 1)
                copy_results(G1 - 1)
                act.wait_ge(back1_done, b + 1)
                nc.scalar.activation(stream[0:64, batch(b, PAD, T)], FB[0:64, :], ACT.Copy).then_inc(stream_in, 1)
                nc.scalar.activation(stream[64:128, batch(b, PAD + 1, T)], FB[64:128, :], ACT.Copy).then_inc(stream_in, 1)

            attend(0)
            with act.Fori(1, B) as b:
                attend(b)

            act.wait_ge(params_in, 16 * DEPTH * (3 + 2 * NF))

            def step(it, u, tail=False):
                n = it * UNITS + u
                first = isinstance(it, int) and it == 0
                with_b = not (first and u < 1) and not (tail and u > 0)
                with_c = not (first and u < 2) and not (tail and u > 1)
                with_d = not (first and u < 3)

                def values(v2):
                    act.wait_ge(v_done, 2 * n + v2 + 1)
                    need(act, pv_done, n - 3)
                    nc.scalar.activation(vwin[:, u % 4, 2 * v2:2 * v2 + 2, :].rearrange("p w n -> p (w n)"), VB,
                                         ACT.Copy).then_inc(v_copied, 1)

                if with_d:
                    act.wait_ge(ot_done, n - 2)
                    need(act, y_done, n - 4)
                    nc.scalar.activation(oT[:, (u - 3) % 2].rearrange("p h t -> p (h t)"), PO, ACT.Copy).then_inc(ot_copied, 1)
                if not tail:
                    values(0)
                if with_c:
                    act.wait_ge(sub_done, n - 1)
                    need(act, pt_done, n - 3)
                    need(act, sum_done, n - 3)
                    nc.scalar.activation(pr[:, u % 2], sm[:], ACT.Exp).then_inc(exp_done, 1)
                if not tail:
                    act.wait_ge(proj_done, n + 1)
                    need(act, red_done, n)
                    nc.scalar.activation(sq[:].rearrange("p h d -> p (h d)"), QK.rearrange("p a n -> p (a n)"),
                                         ACT.Square).then_inc(sq_done, 1)
                if with_c:
                    act.wait_ge(pt_done, n - 1)
                    need(act, pv_done, n - 2)
                    nc.scalar.activation(pT[:].rearrange("p h t -> p (h t)"), PO, ACT.Copy).then_inc(pt_copied, 1)
                if not tail:
                    values(1)
                if with_b:
                    pj, ph = (u - 1) % UNITS // 2, (u - 1) % 2
                    act.wait_ge(kt_done, n)
                    need(act, s_done, n - 1)
                    nc.scalar.activation(kT[:, ph * HP:(ph + 1) * HP, PAD + pj * P:PAD + (pj + 1) * P],
                                         TR.rearrange("p (h t) -> p h t", t=P), ACT.Copy).then_inc(kt_copied, 1)
                if not tail and not first:
                    ff(it, u, 0)
                if with_b:
                    act.wait_ge(qt_done, n)
                    nc.scalar.activation(qT[:].rearrange("p h t -> p (h t)"), TR, ACT.Copy).then_inc(qt_copied, 1)
                if not first and not tail:
                    ff(it, u, 1)
                    ff(it, u, 2)

            def ff(it, u, spot):
                l = (it - 1) // B
                if (u, spot) == (3, 1):
                    act.wait_ge(dev_done, it)
                    nc.scalar.activation(fsq[:], fd[:], ACT.Square).then_inc(fsq_done, 1)
                if (u, spot) == (4, 2):
                    act.wait_ge(xn_done, it)
                    nc.scalar.activation(fxa[:], fxn[:], ACT.Identity, scale=lng[:, bass.ds(l, 1)],
                                         bias=lnb[:, bass.ds(l, 1)]).then_inc(xa_done, 1)
                if u == 5:
                    c = spot
                    m = FCH[c]
                    act.wait_ge(gate_done, (it - 1) * NF + c + 1)
                    nc.scalar.activation(fg[0:m, c, :], FB[0:m, :], ACT.Gelu,
                                         bias=b1g[0:m, c, bass.ds(l, 1)]).then_inc(gelu_done, 1)

            for u in range(UNITS):
                step(0, u)
            with act.Fori(1, ITERS) as it:
                for u in range(UNITS):
                    step(it, u)
            for u in range(3):
                step(ITERS, u, tail=True)
            for u in range(3, UNITS):
                for spot in range(3):
                    ff(ITERS, u, spot)
            def finish(b):
                act.wait_ge(ff_added, 2 * ITERS)
                need(act, back_done, b)
                nc.scalar.activation(fd[0:64, :], stream[0:64, batch(b, PAD, T)], ACT.Copy).then_inc(flat_done, 1)
                nc.scalar.activation(fd[64:128, :], stream[64:128, batch(b, PAD + 1, T)], ACT.Copy).then_inc(flat_done, 1)

            finish(0)
            with act.Fori(1, B) as b:
                finish(b)

        @block.vector
        def _(dve):
            dve.wait_ge(consts_in, 16 * N_CONST)
            def attend(b):
                for m in range(2 * G1):
                    i, g = m % 2, m // 2
                    dve.wait_ge(hi1_done, b * (2 * G1) + m + 1)
                    nc.vector.scalar_tensor_tensor(out=qk1[:, i, g, :], in0=qk1[:, i, g, :], scalar=parts[:, i:i + 1],
                                                   in1=banks[:, m % 4, :], op0=ALU.mult, op1=ALU.add).then_inc(lo1_done, 1)

                def maxima(g, x):
                    i, half = x // 2, x % 2
                    h = g * GH + 2 * half
                    dve.wait_ge(s1_done, b * (G1 * MAXES) + g * MAXES + x + 1)
                    nc.vector.tensor_reduce(mx1[:, i, h:h + 2], banks[:, 2 * half:2 * half + 2, 0:(i + 1) * P], AX.X,
                                            ALU.max).then_inc(mx1_done, 1)

                def place(g):
                    dve.wait_ge(mx1_done, b * (G1 * MAXES) + (g + 1) * MAXES)
                    need(dve, mt1_done, b * G1)
                    nc.vector.tensor_scalar(mnat[:, :, g * GH:(g + 1) * GH, MAXROW], mx1[:, :, g * GH:(g + 1) * GH], -1.0,
                                            None, ALU.mult).then_inc(neg1_done, 1)

                def join(g):
                    dve.wait_ge(mt1_done, b * G1 + g + 1)
                    need(dve, st1_done, b * (QUADS * GH) + max(g - 1, 0) * (NT * GH))
                    nc.vector.tensor_tensor(qm1[:, g % 2, :], FB.bitcast(F16)[:, 0:T], qk1[:, 0, g, :],
                                            ALU.add).then_inc(qm1_done, 1)

                def divide(g):
                    dve.wait_ge(on1_done, b * G1 + g + 1)
                    if g == 0:
                        need(dve, back1_done, b)
                    turned = FB.rearrange("p (t r s) -> p t r s", t=NT, s=SLOT)
                    nc.vector.reciprocal(rl1[:].rearrange("p (t r) -> p t r", t=NT), turned[:, :, :, D1]).then_inc(rl1_done, 1)
                    dve.wait_ge(rl1_done, b * G1 + g + 1)
                    nc.vector.tensor_tensor(y1[:].rearrange("p t (h d) -> p t h d", d=D1)[:, :, g * GH:(g + 1) * GH, :],
                                            turned[:, :, :, 0:D1],
                                            rl1[:].rearrange("p (t r) -> p t r", t=NT).unsqueeze(3).broadcast_to([P, NT, GH, D1]),
                                            ALU.mult).then_inc(part1_done, 1)

                for x in range(MAXES):
                    maxima(0, x)
                place(0)
                join(0)
                for g in range(G1):
                    if g + 1 < G1:
                        for x in range(MAXES):
                            maxima(g + 1, x)
                            if x == 4 and g:
                                divide(g - 1)
                        place(g + 1)
                        join(g + 1)
                divide(G1 - 2)
                divide(G1 - 1)
                base = b * 5 - 1
                dve.wait_ge(xt1_done, b + 1)
                dve.wait_ge(part1_done, b * G1 + G1)
                nc.vector.tensor_tensor(y1[:], y1[:], xin[:], ALU.add).then_inc(ln1_chain, 1)
                dve.wait_ge(ln1_chain, base + 2)
                for t in range(NT):
                    last = nc.vector.bn_stats(bn[:, t, :], y1[:, t, :])
                last.then_inc(stats1_done, 1)
                plain(dve)
                dve.wait_ge(stats1_done, b + 1)
                for t in range(NT):
                    last = nc.vector.bn_aggr(mv[:, t, :], bn[:, t, :])
                last.then_inc(ln1_chain, 1)
                dve.wait_ge(ln1_chain, base + 3)
                nc.vector.tensor_scalar(vv1[:], mv[:, :, 1], EPS, None, ALU.add).then_inc(ln1_chain, 1)
                dve.wait_ge(rs1_done, b + 1)
                for t in range(NT):
                    last = nc.vector.tensor_scalar(y1[:, t, :], y1[:, t, :], mv[:, t, 0:1], rs1[:, t:t + 1],
                                                   ALU.subtract, ALU.mult)
                last.then_inc(ln1_chain, 1)
                dve.wait_ge(ln1_chain, base + 5)
                nc.vector.tensor_copy(x1[:, bass.ds(b * NT, NT), :], y1[:]).then_inc(ln1_chain, 1)

            attend(0)
            with dve.Fori(1, B) as b:
                attend(b)

            dve.wait_ge(stream_in, 2 * B)
            dve.wait_ge(zeroed, 10)
            dve.wait_ge(params_in, 16 * DEPTH * (3 + 2 * NF))

            def shifted_input(b):
                nc.vector.tensor_copy(xs[:], stream[:, batch(b, 0, PAD + T)]).then_inc(xs_done, 1)

            def step(it, u, tail=False):
                n = it * UNITS + u
                first = isinstance(it, int) and it == 0
                with_b = not (first and u < 1) and not (tail and u > 0)
                with_c = not (first and u < 2) and not (tail and u > 1)
                with_d = not (first and u < 3)
                if with_c:
                    dve.wait_ge(s_done, n - 1)
                    nc.vector.tensor_reduce(mx[:], SB_.rearrange("p (h k) -> p h k", k=2 * WIN), AX.X,
                                            ALU.max).then_inc(max_done, 1)
                    dve.wait_ge(max_done, n - 1)
                    need(dve, exp_done, n - 2)
                    nc.vector.tensor_tensor(sm[:], SB_.rearrange("p (h k) -> p h k", k=2 * WIN),
                                            mx[:].unsqueeze(2).broadcast_to([P, HH, 2 * WIN]),
                                            ALU.subtract).then_inc(sub_done, 1)
                if with_b:
                    dve.wait_ge(norm_qk, n)
                    need(dve, tab_done, (it + 1) if u else it)
                    nc.vector.tensor_tensor(qkc[:].rearrange("p (a h) d -> p a h d", a=2),
                                            qkn[:].rearrange("p (a h) d -> p a h d", a=2),
                                            tab[:, 2 * ((u - 1) % UNITS // 2), :].rearrange("p (a o d) -> p a o d", a=2, o=1)
                                            .broadcast_to([P, 2, HH, D]),
                                            ALU.mult).then_inc(cos_done, 1)
                    dve.wait_ge(cos_done, n)
                    dve.wait_ge(sin_done, n)
                    need(dve, qt_done, n - 1)
                    nc.vector.tensor_tensor(qkr[:].rearrange("p h (t f) -> p h t f", t=2),
                                            qkc[:].rearrange("p h (t f) -> p h t f", t=2),
                                            qks_[:].rearrange("p h (t f) -> p h t f", t=2)[:, :, ::-1, :],
                                            ALU.add).then_inc(rot_done, 1)
                if not tail:
                    dve.wait_ge(sq_done, n + 1)
                    nc.vector.tensor_reduce(ss[:], sq[:], AX.X, ALU.add).then_inc(red_done, 1)
                    dve.wait_ge(red_done, n + 1)
                    need(dve, rn_done, n)
                    nc.vector.tensor_scalar(cl[:], ss[:], 1e-24, None, ALU.max).then_inc(clamp_done, 1)
                if with_c:
                    dve.wait_ge(exp_done, n - 1)
                    nc.vector.tensor_reduce(lsum[:], pr[:, u % 2], AX.X, ALU.add).then_inc(sum_done, 1)
                    dve.wait_ge(sum_done, n - 1)
                    if u == UNITS - 1:
                        dve.wait_ge(v_done, 2 * n + 2)
                    nc.vector.reciprocal(rl[:], lsum[:]).then_inc(rl_done, 1)
                if not tail:
                    if u == UNITS - 1:
                        plain(dve)
                        shifted_input((it + 1) % B)
                    if not first:
                        ff(it, u, 0)
                        ff(it, u, 1)
                if with_c:
                    dve.wait_ge(rl_done, n - 1)
                    dve.wait_ge(pv_done, n - 1)
                    need(dve, ot_done, n - 2)
                    nc.vector.tensor_tensor(on[:], OB.rearrange("p (h d) -> p h d", d=D),
                                            rl[:].unsqueeze(2).broadcast_to([P, HH, D]), ALU.mult).then_inc(o_done, 1)
                if not tail:
                    dve.wait_ge(rn_done, n + 1)
                    dve.wait_ge(proj_done, n + 1)
                    need(dve, sin_done, n)
                    need(dve, cos_done, n)
                    nc.vector.tensor_tensor(qkn[:], QK.rearrange("p a (h d) -> p (a h) d", d=D),
                                            rn[:].unsqueeze(2).broadcast_to([P, 2 * HH, D]), ALU.mult).then_inc(norm_qk, 1)
                if with_d:
                    bb = (it if u >= 3 else it - 1) % B
                    at = PAD + (u - 3) % UNITS // 2 * P
                    dve.wait_ge(y_done, n - 2)
                    lo, hi = stream[0:64, batch(bb, at, P)], stream[64:128, batch(bb, at + 1, P)]
                    nc.vector.tensor_tensor(lo, TR[0:64, 0:P], lo, ALU.add).then_inc(y_added, 1)
                    nc.vector.tensor_tensor(hi, TR[64:128, 0:P], hi, ALU.add).then_inc(y_added, 1)
                if not first and not tail:
                    ff(it, u, 2)

            def ff(it, u, spot):
                bb, l = (it - 1) % B, (it - 1) // B
                if (u, spot) == (3, 0):
                    dve.wait_ge(mean_done, it)
                    dve.wait_ge(y_added, it * (2 * UNITS))
                    nc.vector.tensor_tensor(fd[:], stream[:, batch(bb, PAD, T)], FB, ALU.subtract).then_inc(dev_done, 1)
                if (u, spot) == (3, 2):
                    dve.wait_ge(var_done, it)
                    nc.vector.tensor_scalar(fv[:], FB[:, 0:NT], EPS, None, ALU.add).then_inc(fv_done, 1)
                if (u, spot) == (4, 0):
                    dve.wait_ge(frs_done, it)
                    nc.vector.tensor_tensor(fdg[:], ident[:].unsqueeze(1).broadcast_to([P, NT, P]),
                                            frs[:].unsqueeze(2).broadcast_to([P, NT, P]), ALU.mult).then_inc(dg_done, 1)
                if (u, spot) == (4, 2):
                    dve.wait_ge(bc_done, it)
                    nc.vector.tensor_tensor(fxn[:], fd[:], FB, ALU.mult).then_inc(xn_done, 1)
                if u == 6:
                    c = spot
                    m = FCH[c]
                    dve.wait_ge(up_done, (it - 1) * NF + c + 1)
                    dve.wait_ge(gelu_done, (it - 1) * NF + c + 1)
                    nc.vector.scalar_tensor_tensor(out=fh[0:m, c, :], in0=FB[0:m, :], scalar=b1a[0:m, c, bass.ds(l, 1)],
                                                   in1=fg[0:m, c, :], op0=ALU.add, op1=ALU.mult).then_inc(h_done, 1)
                if (u, spot) == (7, 0):
                    dve.wait_ge(down_done, it)
                    lo, hi = stream[0:64, batch(bb, PAD, T)], stream[64:128, batch(bb, PAD + 1, T)]
                    nc.vector.scalar_tensor_tensor(out=lo, in0=FB[0:64, :], scalar=b2[0:64, bass.ds(l, 1)], in1=lo,
                                                   op0=ALU.add, op1=ALU.add).then_inc(ff_added, 1)
                    nc.vector.scalar_tensor_tensor(out=hi, in0=FB[64:128, :], scalar=b2[64:128, bass.ds(l, 1)], in1=hi,
                                                   op0=ALU.add, op1=ALU.add).then_inc(ff_added, 1)

            shifted_input(0)
            for u in range(UNITS):
                step(0, u)
            with dve.Fori(1, ITERS) as it:
                for u in range(UNITS):
                    step(it, u)
            for u in range(3):
                step(ITERS, u, tail=True)
            for u in range(3, UNITS):
                for spot in range(3):
                    ff(ITERS, u, spot)
            def finish(b):
                dve.wait_ge(back_done, b + 1)
                need(dve, stored, b * 16)
                nc.vector.tensor_tensor(y1[:], FB.rearrange("p (t c) -> p t c", c=C), x1[:, bass.ds(b * NT, NT), :],
                                        ALU.add).then_inc(fin_sum, 1)
                dve.wait_ge(fin_sum, b + 1)
                for t in range(NT):
                    last = nc.vector.bn_stats(bn[:, t, :], y1[:, t, :])
                last.then_inc(fin_stats, 1)
                plain(dve)
                dve.wait_ge(fin_stats, b + 1)
                for t in range(NT):
                    last = nc.vector.bn_aggr(mv[:, t, :], bn[:, t, :])
                last.then_inc(fin_aggr, 1)
                dve.wait_ge(fin_aggr, b + 1)
                nc.vector.tensor_scalar(vv1[:], mv[:, :, 1], EPS, None, ALU.add).then_inc(fin_var, 1)
                dve.wait_ge(fin_rs, b + 1)
                for t in range(NT):
                    last = nc.vector.tensor_scalar(y1[:, t, :], y1[:, t, :], mv[:, t, 0:1], rs1[:, t:t + 1],
                                                   ALU.subtract, ALU.mult)
                last.then_inc(fin_done, 1)

            finish(0)
            with dve.Fori(1, B) as b:
                finish(b)

        @block.tensor
        def _(pe):
            def turn(dst, src):
                return nc.tensor.transpose(dst, src, ident[:])

            pe.wait_ge(consts_in, 16 * N_CONST)
            pe.wait_ge(w1nat_in, 48)
            for i in range(3):
                last = turn(FB[:, i * C:(i + 1) * C], w1nat[:, i, :])
            last.then_inc(wt_done, 1)
            pe.wait_ge(wt_copied, 7)
            pe.wait_ge(bf_ready, 3)
            def attend(b):
                pe.wait_ge(xin_in, b * 16 + 16)
                need(pe, stream_in, b * 2)
                for t in range(NT):
                    last = turn(FB[:, t * P:(t + 1) * P], xin[:, t, :])
                last.then_inc(xt1_done, 1)
                pe.wait_ge(xt1_copied, b + 1)
                for m in range(2 * G1):
                    i, g = m % 2, m // 2
                    if m < 4:
                        need(pe, mx1_done, b * (G1 * MAXES))
                    else:
                        pe.wait_ge(lo1_done, b * (2 * G1) + m - 3)
                    w = (wq1, wk1)[i]
                    nc.tensor.matmul(banks[:, m % 4, :], w[:, g * (P // SLOT):(g + 1) * (P // SLOT), :].rearrange("p h s -> p (h s)"),
                                     x1t[:], start=True, stop=True).then_inc(pj1_done, 1)
                for t in range(NT):
                    last = nc.tensor.matmul(FB[:, t * C:(t + 1) * C], x1t[:, t * P:(t + 1) * P], wv1[:], start=True, stop=True)
                last.then_inc(v1_done, 1)
                pe.wait_ge(lo1_done, (b + 1) * (2 * G1))

                def scores(g, x):
                    i, half = x // 2, x % 2
                    need(pe, mx1_done, b * (G1 * MAXES) + g * MAXES + x - 1)
                    for r in range(2 * half, 2 * half + 2):
                        at = r * SLOT
                        nc.tensor.matmul(banks[:, r, 0:(i + 1) * P], qk1[at:at + SLOT, 0, g, i * P:(i + 1) * P],
                                         qk1[at:at + SLOT, 1, g, 0:(i + 1) * P], start=True, stop=False,
                                         tile_position=(at, 0))
                        last = nc.tensor.matmul(banks[:, r, i * P:(i + 1) * P], identb[:], maskb[:, 4 * WIN:4 * WIN + P],
                                                start=False, stop=True)
                    last.then_inc(s1_done, 1)

                def turn_maxima(g):
                    if g == 0:
                        pe.wait_ge(v1_copied, b + 1)
                    elif g >= 2:
                        pe.wait_ge(part1_done, b * G1 + g - 1)
                    pe.wait_ge(neg1_done, b * G1 + g + 1)
                    for i in range(NT):
                        last = nc.tensor.transpose(FB.bitcast(F16)[:, i * P:(i + 1) * P],
                                                   mnat[:, i, g * GH:(g + 1) * GH, :].rearrange("p r s -> p (r s)"), identh[:])
                    last.then_inc(mt1_done, 1)

                def shifted(q, r):
                    g, k = q // NT, q % NT
                    e = (b * QUADS + q) * GH + r
                    at = r * SLOT
                    need(pe, exp1_done, e - 1)
                    if k == 0:
                        pe.wait_ge(qm1_done, b * G1 + g + 1)
                    nc.tensor.matmul(banks[:, 4 + r % 2, 0:T - k * P], qk1[at:at + SLOT, 1, g, k * P:(k + 1) * P],
                                     qm1[at:at + SLOT, g % 2, k * P:T], start=True, stop=False, tile_position=(at, 0))
                    nc.tensor.matmul(banks[:, 4 + r % 2, 0:P], identb[:], maskb[:, 4 * WIN + P:4 * WIN + 2 * P],
                                     start=False, stop=True).then_inc(st1_done, 1)

                def results(q):
                    g, k = q // NT, q % NT
                    n = b * QUADS + q
                    pe.wait_ge(exp1_done, n * GH + GH)
                    if k == 0:
                        need(pe, ot1_copied, b * G1 + g)
                    for r in range(GH):
                        last = nc.tensor.matmul(banks[SLOT * r:SLOT * r + SLOT, 6, k * P:T], v1[:, k, g * GH + r, :],
                                                p1[:, q % 2, r, 0:T - k * P], start=(k == 0), stop=(k == NT - 1),
                                                tile_position=(0, SLOT * r), skip_group_check=True)
                    last.then_inc(pv1_done, 1)

                def turn_results(g):
                    pe.wait_ge(ot1_copied, b * G1 + g + 1)
                    if g + 1 < G1:
                        pe.wait_ge(qm1_done, b * G1 + g + 2)
                    else:
                        pe.wait_ge(part1_done, b * G1 + g)
                    for i in range(NT):
                        last = turn(FB[:, i * P:(i + 1) * P], ot1[:, i * P:(i + 1) * P])
                    last.then_inc(on1_done, 1)

                for x in range(MAXES):
                    scores(0, x)
                turn_maxima(0)
                for q in range(QUADS):
                    g, k = q // NT, q % NT
                    if g + 1 < G1:
                        scores(g + 1, 2 * k)
                    shifted(q, 0)
                    shifted(q, 1)
                    if q:
                        results(q - 1)
                    if g + 1 < G1:
                        scores(g + 1, 2 * k + 1)
                    shifted(q, 2)
                    shifted(q, 3)
                    if g and k == 1:
                        turn_results(g - 1)
                    if g + 1 < G1 and k == NT - 1:
                        turn_maxima(g + 1)
                results(QUADS - 1)
                turn_results(G1 - 1)
                pe.wait_ge(ln1_chain, b * 5 + 4)
                pe.wait_ge(part1_done, b * G1 + G1)
                for t in range(NT):
                    last = turn(FB[:, t * P:(t + 1) * P], y1[:, t, :])
                last.then_inc(back1_done, 1)

            attend(0)
            with pe.Fori(1, B) as b:
                attend(b)

            pe.wait_ge(stream_in, 2 * B)

            def step(it, u, tail=False):
                n = it * UNITS + u
                first = isinstance(it, int) and it == 0
                j, hf = u // 2, u % 2
                pj, ph = (u - 1) % UNITS // 2, (u - 1) % 2
                with_b = not (first and u < 1) and not (tail and u > 0)
                with_c = not (first and u < 2) and not (tail and u > 1)
                with_d = not (first and u < 3)
                wv = wqkv[:, 2 * INNER + hf * 512:2 * INNER + (hf + 1) * 512].rearrange("p (h r d) -> p r h d", r=2, d=D)

                def values(v2):
                    need(pe, v_copied, 2 * n + v2)
                    for w in range(2 * v2, 2 * v2 + 2):
                        for r in range(2):
                            at = j * P + w * WIN
                            last = nc.tensor.matmul(VB[64 * r:64 * r + 64, (w % 2) * 256:(w % 2 + 1) * 256].rearrange("p (h d) -> p h d", d=D),
                                                    xs[:, at:at + 2 * WIN], wv[:, r], start=True, stop=True,
                                                    tile_position=(0, 64 * r))
                    last.then_inc(v_done, 1)

                def scores(par):
                    r = 64 * par
                    for h in range(par, HH, 2):
                        for w in range(NW):
                            at = pj * P + w * WIN
                            last = nc.tensor.matmul(SB_[32 * w:32 * w + 32, h * 2 * WIN:(h + 1) * 2 * WIN],
                                                    qT[r:r + 64, h // 2, 32 * w:32 * w + 32],
                                                    kT[r:r + 64, ph * HP + h // 2, at:at + 2 * WIN],
                                                    start=False, stop=True, tile_position=(r, 32 * w),
                                                    skip_group_check=True)
                    return last

                def results(par):
                    r = 64 * par
                    for h in range(par, HH, 2):
                        for w in range(NW):
                            last = nc.tensor.matmul(OB[32 * w:32 * w + 32, h * D:(h + 1) * D],
                                                    pT[r:r + 64, h // 2, 32 * w:32 * w + 32],
                                                    vwin[r:r + 64, (u - 2) % 4, w, h // 2 * D:(h // 2 + 1) * D],
                                                    start=True, stop=True, tile_position=(r, 32 * w))
                    return last

                if with_d:
                    pe.wait_ge(o_done, n - 2)
                    need(pe, pt_copied, n - 2)
                    for h in range(HP):
                        last = turn(PO[:, h * P:(h + 1) * P], on[:, 2 * h:2 * h + 2, :].rearrange("p h d -> p (h d)"))
                    last.then_inc(ot_done, 1)
                if not tail:
                    if u == 0:
                        pe.wait_ge(wqkv_in, (it // B) * 16 + 16)
                        pe.wait_ge(xs_done, it + 1)
                    values(0)
                    need(pe, norm_qk, n)
                    need(pe, sq_done, n)
                    for i in range(2):
                        last = nc.tensor.matmul(QK[:, i, :], xs[:, PAD + j * P:PAD + (j + 1) * P],
                                                wqkv[:, i * INNER + hf * 512:i * INNER + hf * 512 + 512], start=True, stop=True)
                    last.then_inc(proj_done, 1)
                    if not first:
                        ff(it, u, 0)
                if with_c:
                    pe.wait_ge(exp_done, n - 1)
                    need(pe, ot_copied, n - 2)
                    for h in range(HP):
                        last = turn(PO[:, h * P:(h + 1) * P], pr[:, u % 2, 2 * h:2 * h + 2, :].rearrange("p h d -> p (h d)"))
                    last.then_inc(pt_done, 1)
                if not tail:
                    values(1)
                if with_b:
                    pe.wait_ge(rot_done, n)
                    need(pe, qt_copied, n - 1)
                    need(pe, y_added, 2 * (n - 3))
                    for h in range(HP):
                        last = turn(TR[:, h * P:(h + 1) * P], qkr[:, HH + 2 * h:HH + 2 * h + 2, :].rearrange("p h d -> p (h d)"))
                    last.then_inc(kt_done, 1)
                if with_c:
                    plain(pe)
                    pe.wait_ge(pt_copied, n - 1)
                    need(pe, o_done, n - 2)
                    results(1).then_inc(pv_odd, 1)
                if with_b:
                    pe.wait_ge(kt_copied, n)
                    for h in range(HP):
                        last = turn(TR[:, h * P:(h + 1) * P], qkr[:, 2 * h:2 * h + 2, :].rearrange("p h d -> p (h d)"))
                    last.then_inc(qt_done, 1)
                    need(pe, sub_done, n - 1)
                    m = maskb[:, 0:2 * WIN] if pj else maskb[:, 2 * WIN:4 * WIN]
                    nc.tensor.matmul(SB_.rearrange("p (h k) -> p h k", k=2 * WIN), identb[:],
                                     m.unsqueeze(1).broadcast_to([P, HH, 2 * WIN]), start=True, stop=False,
                                     skip_group_check=True)
                if with_c:
                    plain(pe)
                    pe.wait_ge(pv_odd, n - 1)
                    results(0).then_inc(pv_done, 1)
                if not first and not tail:
                    ff(it, u, 1)
                if with_b:
                    plain(pe)
                    pe.wait_ge(qt_copied, n)
                    scores(0).then_inc(s_even, 1)
                if with_d:
                    if u == 3:
                        pe.wait_ge(wo_in, (it // B) * 16 + 16)
                    pe.wait_ge(ot_copied, n - 2)
                    pe.wait_ge(qt_copied, min(n, ITERS * UNITS) if tail else n)
                    if tail:
                        pe.wait_ge(y_added, 2 * (n - 3))
                    for h in range(HP):
                        last = nc.tensor.matmul(TR[:, 0:P], wo[:, (u - 3) % 2 * HP + h, :], oT[:, (u - 3) % 2, h, :],
                                                start=(h == 0), stop=(h == HP - 1))
                    last.then_inc(y_done, 1)
                if with_b:
                    plain(pe)
                    pe.wait_ge(s_even, n)
                    scores(1).then_inc(s_done, 1)
                if not first and not tail:
                    ff(it, u, 2)

            def ff(it, u, spot):
                bb, l = (it - 1) % B, (it - 1) // B
                if (u, spot) == (3, 0):
                    pe.wait_ge(y_added, it * (2 * UNITS))
                    nc.tensor.matmul(FB, mean_w[:], stream[:, batch(bb, PAD, T)], start=True, stop=True).then_inc(mean_done, 1)
                if (u, spot) == (3, 2):
                    pe.wait_ge(fsq_done, it)
                    for t in range(NT):
                        last = nc.tensor.matmul(FB[:, t:t + 1], fsq[:, t * P:(t + 1) * P], mean_w[:, 0:1], start=True, stop=True)
                    last.then_inc(var_done, 1)
                if (u, spot) == (4, 1):
                    pe.wait_ge(dg_done, it)
                    nc.tensor.matmul(FB, ones[:], fdg[:].rearrange("p t c -> p (t c)"), start=True, stop=True).then_inc(bc_done, 1)
                if u == 5:
                    c = spot
                    m = FCH[c]
                    if c == 0:
                        pe.wait_ge(w1_in, l * 16 + 16)
                        pe.wait_ge(xa_done, it)
                    else:
                        pe.wait_ge(gelu_done, (it - 1) * NF + c)
                    nc.tensor.matmul(FB[0:m, :], w1[:, FF + c * P:FF + c * P + m], fxa[:], start=True, stop=True).then_inc(gate_done, 1)
                if u == 6:
                    c = spot
                    m = FCH[c]
                    if c == 0:
                        pe.wait_ge(gelu_done, it * NF)
                    else:
                        pe.wait_ge(h_done, (it - 1) * NF + c)
                    nc.tensor.matmul(FB[0:m, :], w1[:, c * P:c * P + m], fxa[:], start=True, stop=True).then_inc(up_done, 1)
                if (u, spot) == (7, 0):
                    pe.wait_ge(h_done, it * NF)
                    pe.wait_ge(w2_in, l * (16 * NF) + 16 * NF)
                    for c in range(NF):
                        m = FCH[c]
                        last = nc.tensor.matmul(FB, w2[0:m, c, :], fh[0:m, c, :], start=(c == 0), stop=(c == NF - 1))
                    last.then_inc(down_done, 1)

            for u in range(UNITS):
                step(0, u)
            with pe.Fori(1, ITERS) as it:
                for u in range(UNITS):
                    step(it, u)
            for u in range(3):
                step(ITERS, u, tail=True)
            for u in range(3, UNITS):
                for spot in range(3):
                    ff(ITERS, u, spot)
            def finish(b):
                pe.wait_ge(flat_done, b * 2 + 2)
                need(pe, fin_sum, b)
                for t in range(NT):
                    last = turn(FB[:, t * P:(t + 1) * P], fd[:, t * P:(t + 1) * P])
                last.then_inc(back_done, 1)

            finish(0)
            with pe.Fori(1, B) as b:
                finish(b)


_INS = ['L0_attn_x', 'L0_attn_Wq', 'L0_attn_Wk', 'L0_attn_Wv', 'L0_ffn_Wqkv', 'L0_ffn_q_scale', 'L0_ffn_k_scale',
        'L0_ffn_Wo', 'L0_ffn_ln_g', 'L0_ffn_ln_b', 'L0_ffn_W1', 'L0_ffn_b1', 'L0_ffn_W2', 'L0_ffn_b2']
_CONSTS = ['rot', 'masks', 'ident', 'parts']


def kernel(**inputs):
    import numpy as _np
    import concourse.bacc as _bacc
    from concourse import mybir as _mybir
    from concourse.bass_utils import run_bass_kernel_spmd as _run

    nc = _bacc.Bacc("TRN2", target_bir_lowering=False, num_devices=1)
    arrays, args = {}, []
    consts = constants()
    for name in _INS + _CONSTS:
        a = _np.ascontiguousarray(inputs[name] if name in _INS else consts[name])
        arrays[f"in_{name}_dram"] = a
        args.append(nc.dram_tensor(f"in_{name}_dram", a.shape, _mybir.dt.from_np(a.dtype), kind="ExternalInput").ap())
    args.append(nc.dram_tensor("out_0_dram", (B, T, C), _mybir.dt.float32, kind="ExternalOutput").ap())
    build(nc, *args)
    r = _run(nc, [arrays], core_ids=[0])
    return r.results[0]["out_0_dram"]
```

```python
from contextlib import ExitStack

import concourse.bass as bass
import numpy as np
from concourse import mybir

ALU = mybir.AluOpType
ACT = mybir.ActivationFunctionType
AX = mybir.AxisListType
F32 = mybir.dt.float32
F16 = mybir.dt.float16
BF16 = mybir.dt.bfloat16

P = 128
B, T, C = 8, 512, 128
NT = T // P
H1 = 16
D1 = C // H1
SLOT = 32
G1 = H1 * SLOT // P
SCALE1 = float(C) ** -0.5
GH = P // SLOT
MAXROW = 3 * D1
MAXES = 2 * NT
QUADS = G1 * NT
AHEAD = (((), (0, 1)), ((2,), (3,)), ((4,), (5,)), ((6,), (7,)))
DEPTH = 6
H, D, WIN = 16, 64, 32
INNER = H * D
QK_SCALE = 8.0
HH = H // 2
HP = HH // 2
NW = P // WIN
UNITS = NT * 2
ITERS = DEPTH * B
FF = C * 4 * 2 // 3
FCH = [min(P, FF - c * P) for c in range(-(-FF // P))]
NF = len(FCH)
PAD = WIN
COLS = PAD + T + 4
EPS = 1e-5
NEG = -1e30


def constants():
    f = np.float32
    half = np.arange(0, D, 2, dtype=f)
    inv_freq = f(1.0) / f(10000.0) ** (half / f(D))
    t = np.arange(T, dtype=f)
    freqs = t[:, None] * inv_freq[None, :]
    base = (half + f(0.4 * D)) / f(1.4 * D)
    power = (t - T // 2) / f(WIN // 2)
    scale = base[None, :] ** power[:, None]
    cos, sin = np.cos(freqs), np.sin(freqs)
    rows = np.zeros((T, 2, 2, D), f)
    for i, s in enumerate((scale * f(QK_SCALE), f(1.0) / scale)):
        rows[:, 0, i, :] = np.concatenate([cos * s, cos * s], -1)
        rows[:, 1, i, :] = np.concatenate([sin * s, -sin * s], -1)
    rot = rows.reshape(NT, P, 4 * D).transpose(1, 0, 2).reshape(P, NT * 4 * D)
    q = np.arange(P)[:, None] % WIN + WIN
    k = np.arange(2 * WIN)[None, :]
    mask = np.where((q < k) | (q > k + WIN), f(NEG), f(0.0))
    first = mask.copy()
    first[:WIN, :WIN] = NEG
    causal = np.where(np.arange(P)[:, None] < np.arange(P)[None, :], f(NEG), f(0.0))
    row = np.arange(P)[:, None] % SLOT // D1
    at_max = np.arange(P)[:, None] % SLOT == MAXROW
    slots = np.arange(P)[:, None] // SLOT == np.arange(P // SLOT)[None, :]
    parts = np.concatenate([-(row == 1).astype(f), at_max.astype(f) - (row == 2), at_max.astype(f), slots], 1).astype(f)
    return {
        "rot": np.ascontiguousarray(rot.astype(f)),
        "masks": np.ascontiguousarray(np.concatenate([mask, first, causal, causal.T], 1).astype(f)),
        "ident": np.eye(P, dtype=f),
        "parts": np.ascontiguousarray(parts),
    }


def need(eng, sem, value):
    if isinstance(value, int) and value <= 0:
        return
    eng.wait_ge(sem, value)


def build(nc, x, wq1_d, wk1_d, wv1_d, wqkv_d, qs_d, ks_d, wo_d, lng_d, lnb_d, w1_d, b1_d, w2_d, b2_d,
          rot_d, masks_d, ident_d, parts_d, out):
    with ExitStack() as ctx:
        def sb(name, shape, dt=F32):
            return ctx.enter_context(nc.sbuf_tensor(name, shape, dt))

        def sem(name):
            return ctx.enter_context(nc.semaphore(name))

        stream = sb("stream", [P, B * COLS])
        x1 = sb("x1", [P, B * NT, C])
        ident = sb("ident", [P, P])
        identb = sb("identb", [P, P], BF16)
        identh = sb("identh", [P, P], F16)
        masks = sb("masks", [P, 4 * WIN + 2 * P])
        maskb = sb("maskb", [P, 4 * WIN + 2 * P], BF16)
        ones = sb("ones", [P, P])
        mean_w = sb("mean_w", [P, P])
        neghalf = sb("neghalf", [P, H])
        parts = sb("parts", [P, 3 + GH])
        w1nat = sb("w1nat", [P, 3, C])
        wq1 = sb("wq1", [P, H1, SLOT])
        wk1 = sb("wk1", [P, H1, SLOT])
        wv1 = sb("wv1", [P, C])
        xin = sb("xin", [P, NT, C])
        x1t = sb("x1t", [P, T])
        qk1 = sb("qk1", [P, 2, G1, T], F16)
        v1 = sb("v1", [P, NT, H1, SLOT])
        mx1 = sb("mx1", [P, NT, H1])
        mnat = sb("mnat", [P, NT, H1, SLOT], F16)
        qm1 = sb("qm1", [P, 2, T], F16)
        p1_vwin = sb("p1_vwin", [P, 2 * GH * T])
        p1 = p1_vwin[:].rearrange("p (a r t) -> p a r t", a=2, r=GH)
        ot1 = sb("ot1", [P, T])
        rl1 = sb("rl1", [P, NT * GH])
        y1 = sb("y1", [P, NT, C])
        bn = sb("bn", [P, NT, 6])
        mv = sb("mv", [P, NT, 2])
        vv1 = sb("vv1", [P, NT])
        rs1 = sb("rs1", [P, NT])
        wqkv = sb("wqkv", [P, 3 * INNER])
        wo = sb("wo", [P, INNER // P, C])
        w1 = sb("w1", [P, 2 * FF])
        w2 = sb("w2", [P, NF, C])
        qks = sb("qks", [P, 2 * D])
        rot = sb("rot", [P, NT * 2, 2 * D])
        tab = sb("tab", [P, NT * 2, 2 * D])
        lng = sb("lng", [P, DEPTH])
        lnb = sb("lnb", [P, DEPTH])
        b1a = sb("b1a", [P, NF, DEPTH])
        b1g = sb("b1g", [P, NF, DEPTH])
        b2 = sb("b2", [P, DEPTH])
        xs = sb("xs", [P, PAD + T])
        heads_qk = sb("heads_qk", [P, 4 * 2 * HH * D])
        sq, qkn, qkc, qks_ = (heads_qk[:, i * 2 * HH * D:(i + 1) * 2 * HH * D].rearrange("p (h d) -> p h d", d=D)
                              for i in range(4))
        kz = heads_qk[:].bitcast(F16).rearrange("p (g r t) -> p g r t", g=G1, r=GH)
        ss = sb("ss", [P, 2 * HH])
        cl = sb("cl", [P, 2 * HH])
        rn = sb("rn", [P, 2 * HH])
        qkr = sb("qkr", [P, 2 * HH, D])
        qT = sb("qT", [P, HP, P])
        kT = sb("kT", [P, 2 * HP, PAD + T])
        vwin = p1_vwin[:].rearrange("p (a w n) -> p a w n", a=4, w=NW)
        mx = sb("mx", [P, HH])
        sm = sb("sm", [P, HH, 2 * WIN])
        pr = sb("pr", [P, 2, HH, 2 * WIN])
        lsum = sb("lsum", [P, HH])
        rl = sb("rl", [P, HH])
        pT = sb("pT", [P, HP, P])
        on = sb("on", [P, HH, D])
        oT = sb("oT", [P, 2, HP, P])
        fd = sb("fd", [P, T])
        fsq = sb("fsq", [P, T])
        fv = sb("fv", [P, NT])
        frs = sb("frs", [P, NT])
        fdg = sb("fdg", [P, NT, P])
        fxn = sb("fxn", [P, T])
        fxa = sb("fxa", [P, T])
        fg = sb("fg", [P, NF, T])
        fh = sb("fh", [P, NF, T])

        ys, flats = (y1, xin), (fd, fsq)

        banks = ctx.enter_context(nc.psum_tensor("banks", [P, 8, 512], F32))
        QK, VB, TR, SB_, PO, OB, FB = banks[:, 0:2, :], banks[:, 2, :], banks[:, 3, :], banks[:, 4, :], \
            banks[:, 5, :], banks[:, 6, :], banks[:, 7, :]

        turned = (FB, OB)

        consts_in, params_in, w1nat_in, xin_in, x1_in = sem("consts_in"), sem("params_in"), sem("w1nat_in"), sem("xin_in"), sem("x1_in")
        wqkv_in, wo_in, w1_in, w2_in, qks_in = sem("wqkv_in"), sem("wo_in"), sem("w1_in"), sem("w2_in"), sem("qks_in")
        zeroed, bf_ready = sem("zeroed"), sem("bf_ready")
        wt_done, wt_copied = sem("wt_done"), sem("wt_copied")
        xt1_done, xt1_copied = sem("xt1_done"), sem("xt1_copied")
        pj1_done, hi1_done, lo1_done, kz_done = sem("pj1_done"), sem("hi1_done"), sem("lo1_done"), sem("kz_done")
        v1_done, v1_copied = sem("v1_done"), sem("v1_copied")
        s1_done, mx1_done, neg1_done, mt1_done, qm1_done = (
            sem("s1_done"), sem("mx1_done"), sem("neg1_done"), sem("mt1_done"), sem("qm1_done"))
        st1_done, exp1_done, pv1_done, ot1_copied, on1_done, rl1_done, part1_done = (
            sem("st1_done"), sem("exp1_done"), sem("pv1_done"), sem("ot1_copied"), sem("on1_done"), sem("rl1_done"),
            sem("part1_done"))
        ln1_chain, stats1_done, rs1_done = sem("ln1_chain"), sem("stats1_done"), sem("rs1_done")
        back1_done, stream_in = sem("back1_done"), sem("stream_in")
        xs_done, proj_done, v_done, sq_done, v_copied = sem("xs_done"), sem("proj_done"), sem("v_done"), sem("sq_done"), sem("v_copied")
        red_done, clamp_done, rn_done, norm_qk, cos_done, sin_done, rot_done, tab_done = (
            sem("red_done"), sem("clamp_done"), sem("rn_done"), sem("norm_qk"), sem("cos_done"), sem("sin_done"), sem("rot_done"), sem("tab_done"))
        kt_done, qt_done, kt_copied, qt_copied = sem("kt_done"), sem("qt_done"), sem("kt_copied"), sem("qt_copied")
        s_even, pv_odd, edge_zeroed = sem("s_even"), sem("pv_odd"), sem("edge_zeroed")
        s_done, max_done, sub_done, exp_done = sem("s_done"), sem("max_done"), sem("sub_done"), sem("exp_done")
        pt_done, pt_copied, pv_done, sum_done, rl_done, o_done = (
            sem("pt_done"), sem("pt_copied"), sem("pv_done"), sem("sum_done"), sem("rl_done"), sem("o_done"))
        ot_done, ot_copied, y_done, y_added = sem("ot_done"), sem("ot_copied"), sem("y_done"), sem("y_added")
        mean_done, dev_done, fsq_done, var_done, fv_done, frs_done, dg_done, bc_done, xn_done, xa_done = (
            sem("mean_done"), sem("dev_done"), sem("fsq_done"), sem("var_done"), sem("fv_done"), sem("frs_done"),
            sem("dg_done"), sem("bc_done"), sem("xn_done"), sem("xa_done"))
        gate_done, gelu_done, up_done, h_done, down_done, ff_added = (
            sem("gate_done"), sem("gelu_done"), sem("up_done"), sem("h_done"), sem("down_done"), sem("ff_added"))
        flat_done, back_done, fin_sum, fin_stats, fin_aggr, fin_var, fin_rs, fin_done, stored = (
            sem("flat_done"), sem("back_done"), sem("fin_sum"), sem("fin_stats"), sem("fin_aggr"), sem("fin_var"), sem("fin_rs"), sem("fin_done"),
            (sem("stored_even"), sem("stored_odd")))

        N_CONST = 4

        def plain(eng):
            eng.wait_ge(consts_in, 16 * N_CONST)

        def batch(b, lo, n):
            return bass.ds(b * COLS + lo, n)

        block = ctx.enter_context(nc.Block())

        @block.sync
        def _(sp):
            sp.dma_start(ident[:], ident_d).then_inc(consts_in, 16)
            sp.dma_start(masks[:], masks_d).then_inc(consts_in, 16)
            sp.dma_start(parts[:], parts_d).then_inc(consts_in, 16)
            for i, w in enumerate((wq1_d, wk1_d, wv1_d)):
                sp.dma_start(w1nat[:, i, :], w).then_inc(w1nat_in, 16)
            sp.dma_start(rot[:].rearrange("p a b -> p (a b)"), rot_d).then_inc(consts_in, 16)

            def load_qkv(l):
                sp.dma_start(wqkv[:], wqkv_d[bass.ds(l, 1)].rearrange("a p n -> p (a n)")).then_inc(wqkv_in, 16)

            def load_scales(l):
                sp.dma_start(qks[:, 0:D], qs_d[bass.ds(l, 1), :].broadcast_to([P, D])).then_inc(qks_in, 16)
                sp.dma_start(qks[:, D:2 * D], ks_d[bass.ds(l, 1), :].broadcast_to([P, D])).then_inc(qks_in, 16)

            def load_out(l):
                sp.dma_start(wo[:], wo_d[bass.ds(l, 1)].rearrange("a (t p) n -> p (a t) n", p=P)).then_inc(wo_in, 16)

            def load_ff(l):
                sp.dma_start(w1[:], w1_d[bass.ds(l, 1)].rearrange("a p n -> p (a n)")).then_inc(w1_in, 16)
                for c in range(NF):
                    sp.dma_start(w2[0:FCH[c], c, :],
                                 w2_d[bass.ds(l, 1), c * P:c * P + FCH[c], :].rearrange("a p n -> p (a n)")
                                 ).then_inc(w2_in, 16)

            def load_x(b):
                sp.dma_start(xin[:], x[bass.ds(b, 1)].rearrange("a (t p) c -> p (a t) c", p=P)).then_inc(xin_in, 16)

            load_x(0)
            sp.dma_start(x1[:], x.rearrange("b (t p) c -> p (b t) c", p=P)).then_inc(x1_in, 16)
            load_qkv(0)
            load_scales(0)
            load_out(0)
            load_ff(0)
            for l in range(DEPTH):
                sp.dma_start(lng[:, l:l + 1], lng_d[l, :].rearrange("(p a) -> p a", a=1)).then_inc(params_in, 16)
                sp.dma_start(lnb[:, l:l + 1], lnb_d[l, :].rearrange("(p a) -> p a", a=1)).then_inc(params_in, 16)
                sp.dma_start(b2[:, l:l + 1], b2_d[l, :].rearrange("(p a) -> p a", a=1)).then_inc(params_in, 16)
                for c in range(NF):
                    for dst, at in ((b1a, 0), (b1g, FF)):
                        sp.dma_start(dst[0:FCH[c], c, l:l + 1],
                                     b1_d[l, at + c * P:at + c * P + FCH[c]].rearrange("(p a) -> p a", a=1)
                                     ).then_inc(params_in, 16)
            with sp.Fori(1, B) as b:
                sp.wait_ge(xt1_done, b)
                load_x(b)
            with sp.Fori(1, DEPTH) as l:
                sp.wait_ge(tab_done, l * B)
                load_scales(l)
                sp.wait_ge(v_done, l * (UNITS * B))
                load_qkv(l)
                sp.wait_ge(y_done, l * (UNITS * B))
                load_out(l)
                sp.wait_ge(down_done, l * B)
                load_ff(l)
            with sp.Fori(0, B // 2) as pair:
                for e in range(2):
                    b = pair * 2 + e
                    sp.wait_ge(fin_done, b + 1)
                    sp.dma_start(out[bass.ds(b, 1)].rearrange("a (t p) c -> p (a t) c", p=P), ys[e][:]).then_inc(stored[e], 16)
            for e in range(2):
                sp.wait_ge(stored[e], B // 2 * 16)

        @block.gpsimd
        def _(pool):
            pool.memset(stream[:], 0.0).then_inc(zeroed, 1)
            pool.memset(kT[:, :, 0:PAD], 0.0).then_inc(zeroed, 1)
            pool.memset(ones[:], 1.0).then_inc(zeroed, 1)
            pool.memset(mean_w[:], 1.0 / C).then_inc(zeroed, 1)
            pool.memset(neghalf[:], -0.5).then_inc(zeroed, 1)
            pool.memset(wq1[:], 0.0).then_inc(zeroed, 1)
            pool.memset(wk1[:], 0.0).then_inc(zeroed, 1)
            pool.memset(v1[:], 0.0).then_inc(zeroed, 1)
            pool.memset(mnat[:], 0.0).then_inc(zeroed, 1)
            pool.wait_ge(zeroed, 9)
            pool.memset(v1[:, :, :, D1:D1 + 1], 1.0).then_inc(zeroed, 1)
            with pool.Fori(0, B) as b:
                pool.wait_ge(ln1_chain, b * 5 + 3)
                pool.tensor_tensor(rs1[:], vv1[:], neghalf[:, 0:NT], ALU.pow).then_inc(rs1_done, 1)

            def step(it, u):
                n = it * UNITS + u
                first = isinstance(it, int) and it == 0
                if u == 0:
                    pool.wait_ge(qks_in, (it // B) * 32 + 32)
                    pool.wait_ge(consts_in, 16 * N_CONST)
                    need(pool, cos_done, n)
                    need(pool, sin_done, n)
                    pool.tensor_tensor(tab[:], rot[:], qks[:].unsqueeze(1).broadcast_to([P, NT * 2, 2 * D]),
                                       ALU.mult).then_inc(tab_done, 1)
                if u == 4 and not first:
                    ff_rstd(it)
                pool.wait_ge(clamp_done, n + 1)
                need(pool, norm_qk, n)
                pool.tensor_tensor(rn[:], cl[:], neghalf[:], ALU.pow).then_inc(rn_done, 1)
                pool.wait_ge(norm_qk, n + 1)
                need(pool, rot_done, n)
                pool.wait_ge(tab_done, it + 1)
                pool.tensor_tensor(qks_.rearrange("p (a h) d -> p a h d", a=2),
                                   qkn.rearrange("p (a h) d -> p a h d", a=2),
                                   tab[:, 2 * (u // 2) + 1, :].rearrange("p (a o d) -> p a o d", a=2, o=1)
                                   .broadcast_to([P, 2, HH, D]),
                                   ALU.mult).then_inc(sin_done, 1)

            def ff_rstd(it):
                pool.wait_ge(fv_done, it)
                pool.tensor_tensor(frs[:], fv[:], neghalf[:, 0:NT], ALU.pow).then_inc(frs_done, 1)

            for u in range(UNITS):
                step(0, u)
            with pool.Fori(1, ITERS) as it:
                for u in range(UNITS):
                    step(it, u)
            ff_rstd(ITERS)
            with pool.Fori(0, B) as b:
                pool.wait_ge(fin_var, b + 1)
                pool.tensor_tensor(rs1[:], vv1[:], neghalf[:, 0:NT], ALU.pow).then_inc(fin_rs, 1)

        @block.scalar
        def _(act):
            act.wait_ge(consts_in, 16 * N_CONST)
            nc.scalar.activation(identb[:], ident[:], ACT.Copy).then_inc(bf_ready, 1)
            nc.scalar.activation(maskb[:], masks[:], ACT.Copy).then_inc(bf_ready, 1)
            nc.scalar.activation(identh[:], ident[:], ACT.Copy).then_inc(bf_ready, 1)
            act.wait_ge(wt_done, 1)
            act.wait_ge(zeroed, 10)
            for i, w in enumerate((wq1, wk1)):
                for r in range(3):
                    nc.scalar.activation(w[:, :, r * D1:(r + 1) * D1],
                                         FB[:, i * C:(i + 1) * C].rearrange("p (h d) -> p h d", d=D1),
                                         ACT.Copy).then_inc(wt_copied, 1)
            nc.scalar.activation(wv1[:], FB[:, 2 * C:3 * C], ACT.Copy).then_inc(wt_copied, 1)
            def turned_input(nb):
                act.wait_ge(xt1_done, nb + 1)
                nc.scalar.activation(x1t[:], banks[:, 0, :], ACT.Copy).then_inc(xt1_copied, 1)

            def high_part(nb, m):
                i, g = m % 2, m // 2
                act.wait_ge(pj1_done, nb * (2 * G1) + m + 1)
                if m == 0:
                    need(act, qm1_done, nb * G1)
                if i:
                    nc.scalar.activation(qk1[:, 1, g, :], banks[:, m % 4, :], ACT.Identity,
                                         bias=parts[:, 2:3]).then_inc(hi1_done, 1)
                else:
                    nc.scalar.activation(qk1[:, 0, g, :], banks[:, m % 4, :], ACT.Copy).then_inc(hi1_done, 1)

            def values1(nb):
                act.wait_ge(v1_done, nb + 1)
                need(act, pv1_done, nb * QUADS)
                nc.scalar.activation(v1[:, :, :, 0:D1], FB.rearrange("p (t h d) -> p t h d", h=H1, d=D1),
                                     ACT.Copy).then_inc(v1_copied, 1)

            def to_stream(b):
                act.wait_ge(back1_done, b + 1)
                nc.scalar.activation(stream[0:64, batch(b, PAD, T)], FB[0:64, :], ACT.Copy).then_inc(stream_in, 1)
                nc.scalar.activation(stream[64:128, batch(b, PAD + 1, T)], FB[64:128, :], ACT.Copy).then_inc(stream_in, 1)

            def attend(b, more):
                def copy_results(g):
                    act.wait_ge(pv1_done, b * QUADS + (g + 1) * NT)
                    need(act, on1_done, b * G1 + g)
                    nc.scalar.activation(ot1[:], banks[:, 6, :], ACT.Copy).then_inc(ot1_copied, 1)

                for q in range(QUADS):
                    g, k = q // NT, q % NT
                    n = b * QUADS + q
                    for r in range(GH):
                        act.wait_ge(st1_done, n * GH + r + 1)
                        if r == 0:
                            need(act, pv1_done, n - 1)
                        nc.scalar.activation(p1[:, q % 2, r, 0:T - k * P], banks[:, 4 + r % 2, 0:T - k * P], ACT.Exp,
                                             scale=SCALE1).then_inc(exp1_done, 1)
                        if more and q == QUADS - NT and r == 1:
                            turned_input(b + 1)
                    if g and k == 0:
                        copy_results(g - 1)
                    if q == 2 and not (isinstance(b, int) and b == 0):
                        to_stream(b - 1)
                    if more and g == G1 - 1:
                        for m in AHEAD[k][0] + AHEAD[k][1]:
                            high_part(b + 1, m)
                copy_results(G1 - 1)
                if more:
                    values1(b + 1)

            turned_input(0)
            for m in range(2 * G1):
                high_part(0, m)
            values1(0)
            attend(0, True)
            with act.Fori(1, B - 1) as b:
                attend(b, True)
            attend(B - 1, False)
            to_stream(B - 1)

            act.wait_ge(params_in, 16 * DEPTH * (3 + 2 * NF))

            def step(it, u, tail=False):
                n = it * UNITS + u
                first = isinstance(it, int) and it == 0
                with_b = not (first and u < 1) and not (tail and u > 0)
                with_c = not (first and u < 2) and not (tail and u > 1)
                with_d = not (first and u < 3)

                def values(r):
                    top, low = slice(64 * r, 64 * r + WIN), slice(64 * r + WIN, 64 * r + 2 * WIN)
                    even, odd = VB[low].rearrange("p (a n) -> p a n", a=2), VB[top].rearrange("p (a n) -> p a n", a=2)
                    slot = vwin[:, u % 4]
                    if r == 0:
                        act.wait_ge(v_done, n + 1)
                        need(act, pv_done, n - 3)
                    nc.scalar.activation(slot[low, 0:NW:2, :], even, ACT.Copy)
                    nc.scalar.activation(slot[low, 1:NW:2, :], odd, ACT.Copy)
                    nc.scalar.activation(slot[top, 1:NW:2, :], even, ACT.Copy)
                    last = nc.scalar.activation(slot[top, 2, :], odd[:, 0, :], ACT.Copy)
                    if r == 0:
                        return
                    if u // 2 < NT - 1:
                        need(act, pv_done, n - 1)
                        for q in range(2):
                            last = nc.scalar.activation(vwin[64 * q:64 * q + WIN, (u + 2) % 4, 0, :],
                                                        VB[64 * q:64 * q + WIN, 256:512], ACT.Copy)
                    last.then_inc(v_copied, 1)

                if with_d:
                    act.wait_ge(ot_done, n - 2)
                    need(act, y_done, n - 4)
                    nc.scalar.activation(oT[:, (u - 3) % 2].rearrange("p h t -> p (h t)"), PO, ACT.Copy).then_inc(ot_copied, 1)
                if with_c:
                    act.wait_ge(sub_done, n - 1)
                    need(act, pt_done, n - 3)
                    need(act, sum_done, n - 3)
                    nc.scalar.activation(pr[:, u % 2], sm[:], ACT.Exp).then_inc(exp_done, 1)
                if not tail:
                    act.wait_ge(proj_done, n + 1)
                    need(act, red_done, n)
                    nc.scalar.activation(sq.rearrange("p h d -> p (h d)"), QK.rearrange("p a n -> p (a n)"),
                                         ACT.Square).then_inc(sq_done, 1)
                if with_c:
                    act.wait_ge(pt_done, n - 1)
                    need(act, pv_done, n - 2)
                    nc.scalar.activation(pT[:].rearrange("p h t -> p (h t)"), PO, ACT.Copy).then_inc(pt_copied, 1)
                if with_b:
                    pj, ph = (u - 1) % UNITS // 2, (u - 1) % 2
                    act.wait_ge(kt_done, n)
                    need(act, s_done, n - 1)
                    nc.scalar.activation(kT[:, ph * HP:(ph + 1) * HP, PAD + pj * P:PAD + (pj + 1) * P],
                                         TR.rearrange("p (h t) -> p h t", t=P), ACT.Copy).then_inc(kt_copied, 1)
                if not tail and not first:
                    ff(it, u, 0)
                if with_b:
                    act.wait_ge(qt_done, n)
                    nc.scalar.activation(qT[:].rearrange("p h t -> p (h t)"), TR, ACT.Copy).then_inc(qt_copied, 1)
                if not tail:
                    values(0)
                    if not first:
                        ff(it, u, 1)
                    values(1)
                    if not first:
                        ff(it, u, 2)

            def ff(it, u, spot):
                l = (it - 1) // B
                if (u, spot) == (3, 1):
                    act.wait_ge(dev_done, it)
                    nc.scalar.activation(fsq[:], fd[:], ACT.Square).then_inc(fsq_done, 1)
                if (u, spot) == (4, 2):
                    act.wait_ge(xn_done, it)
                    nc.scalar.activation(fxa[:], fxn[:], ACT.Identity, scale=lng[:, bass.ds(l, 1)],
                                         bias=lnb[:, bass.ds(l, 1)]).then_inc(xa_done, 1)
                if u == 5:
                    c = spot
                    m = FCH[c]
                    act.wait_ge(gate_done, (it - 1) * NF + c + 1)
                    nc.scalar.activation(fg[0:m, c, :], FB[0:m, :], ACT.Gelu,
                                         bias=b1g[0:m, c, bass.ds(l, 1)]).then_inc(gelu_done, 1)

            for u in range(UNITS):
                step(0, u)
            with act.Fori(1, ITERS) as it:
                for u in range(UNITS):
                    step(it, u)
            for u in range(3):
                step(ITERS, u, tail=True)
            for u in range(3, UNITS):
                for spot in range(3):
                    ff(ITERS, u, spot)
            def finish(b, e):
                act.wait_ge(ff_added, 2 * ITERS)
                need(act, back_done, b - 1)
                nc.scalar.activation(flats[e][0:64, :], stream[0:64, batch(b, PAD, T)], ACT.Copy).then_inc(flat_done, 1)
                nc.scalar.activation(flats[e][64:128, :], stream[64:128, batch(b, PAD + 1, T)], ACT.Copy).then_inc(flat_done, 1)

            finish(0, 0)
            finish(1, 1)
            with act.Fori(1, B // 2) as pair:
                finish(pair * 2, 0)
                finish(pair * 2 + 1, 1)

        @block.vector
        def _(dve):
            dve.wait_ge(consts_in, 16 * N_CONST)
            def low_part(nb, m):
                i, g = m % 2, m // 2
                dve.wait_ge(hi1_done, nb * (2 * G1) + m + 1)
                nc.vector.scalar_tensor_tensor(out=qk1[:, i, g, :], in0=qk1[:, i, g, :], scalar=parts[:, i:i + 1],
                                               in1=banks[:, m % 4, :], op0=ALU.mult, op1=ALU.add).then_inc(lo1_done, 1)

            def single_heads(nb, g):
                dve.wait_ge(lo1_done, nb * (2 * G1) + 2 * g + 2)
                need(dve, st1_done, (nb - 1) * (QUADS * GH) + (g + 1) * (NT * GH))
                for r in range(GH):
                    last = nc.vector.tensor_scalar(kz[:, g, r, :], qk1[:, 1, g, :], parts[:, 3 + r:4 + r], None, ALU.mult)
                last.then_inc(kz_done, 1)

            def maxima(b, g, x):
                i, half = x // 2, x % 2
                h = g * GH + 2 * half
                dve.wait_ge(s1_done, b * (G1 * MAXES) + g * MAXES + x + 1)
                nc.vector.tensor_reduce(mx1[:, i, h:h + 2], banks[:, 2 * half:2 * half + 2, 0:(i + 1) * P], AX.X,
                                        ALU.max).then_inc(mx1_done, 1)

            def place(b, g):
                dve.wait_ge(mx1_done, b * (G1 * MAXES) + (g + 1) * MAXES)
                need(dve, mt1_done, b * G1)
                nc.vector.tensor_scalar(mnat[:, :, g * GH:(g + 1) * GH, MAXROW], mx1[:, :, g * GH:(g + 1) * GH], -1.0,
                                        None, ALU.mult).then_inc(neg1_done, 1)

            def join(b, g):
                dve.wait_ge(mt1_done, b * G1 + g + 1)
                need(dve, st1_done, b * (QUADS * GH) + max(g - 1, 0) * (NT * GH))
                nc.vector.tensor_tensor(qm1[:, g % 2, :], FB.bitcast(F16)[:, 0:T], qk1[:, 0, g, :],
                                        ALU.add).then_inc(qm1_done, 1)

            def divide(b, g):
                dve.wait_ge(on1_done, b * G1 + g + 1)
                if g == 0:
                    need(dve, back1_done, b)
                turned = FB.rearrange("p (t r s) -> p t r s", t=NT, s=SLOT)
                nc.vector.reciprocal(rl1[:].rearrange("p (t r) -> p t r", t=NT), turned[:, :, :, D1]).then_inc(rl1_done, 1)
                dve.wait_ge(rl1_done, b * G1 + g + 1)
                nc.vector.tensor_tensor(y1[:].rearrange("p t (h d) -> p t h d", d=D1)[:, :, g * GH:(g + 1) * GH, :],
                                        turned[:, :, :, 0:D1],
                                        rl1[:].rearrange("p (t r) -> p t r", t=NT).unsqueeze(3).broadcast_to([P, NT, GH, D1]),
                                        ALU.mult).then_inc(part1_done, 1)

            def statistics(b):
                base = b * 5 - 1
                dve.wait_ge(xt1_done, b + 1)
                dve.wait_ge(part1_done, b * G1 + G1)
                dve.wait_ge(x1_in, 16)
                nc.vector.tensor_tensor(y1[:], y1[:], x1[:, bass.ds(b * NT, NT), :], ALU.add).then_inc(ln1_chain, 1)
                dve.wait_ge(ln1_chain, base + 2)
                for t in range(NT):
                    last = nc.vector.bn_stats(bn[:, t, :], y1[:, t, :])
                last.then_inc(stats1_done, 1)
                plain(dve)
                dve.wait_ge(stats1_done, b + 1)
                for t in range(NT):
                    last = nc.vector.bn_aggr(mv[:, t, :], bn[:, t, :])
                last.then_inc(ln1_chain, 1)
                dve.wait_ge(ln1_chain, base + 3)
                nc.vector.tensor_scalar(vv1[:], mv[:, :, 1], EPS, None, ALU.add).then_inc(ln1_chain, 1)

            def norm(b):
                dve.wait_ge(rs1_done, b + 1)
                for t in range(NT):
                    last = nc.vector.tensor_scalar(y1[:, t, :], y1[:, t, :], mv[:, t, 0:1], rs1[:, t:t + 1],
                                                   ALU.subtract, ALU.mult)
                last.then_inc(ln1_chain, 1)
                dve.wait_ge(ln1_chain, b * 5 + 4)
                nc.vector.tensor_copy(x1[:, bass.ds(b * NT, NT), :], y1[:]).then_inc(ln1_chain, 1)

            def attend(b, more):
                for g in range(G1 - 1):
                    for x in range(MAXES):
                        maxima(b, g + 1, x)
                        if x == 2 and g == 0 and not (isinstance(b, int) and b == 0):
                            norm(b - 1)
                        if x == 4 and g:
                            divide(b, g - 1)
                    place(b, g + 1)
                    join(b, g + 1)
                if more:
                    for m in range(2 * G1):
                        low_part(b + 1, m)
                        if m == 2:
                            divide(b, G1 - 2)
                        if m % 2 and m // 2 < G1 - 1:
                            single_heads(b + 1, m // 2)
                    for x in range(MAXES):
                        maxima(b + 1, 0, x)
                        if x == 3:
                            divide(b, G1 - 1)
                    place(b + 1, 0)
                    join(b + 1, 0)
                    single_heads(b + 1, G1 - 1)
                else:
                    divide(b, G1 - 2)
                    divide(b, G1 - 1)
                statistics(b)

            for m in range(2 * G1):
                low_part(0, m)
                if m % 2:
                    single_heads(0, m // 2)
            for x in range(MAXES):
                maxima(0, 0, x)
            place(0, 0)
            join(0, 0)
            attend(0, True)
            with dve.Fori(1, B - 1) as b:
                attend(b, True)
            attend(B - 1, False)
            norm(B - 1)

            dve.wait_ge(stream_in, 2 * B)
            dve.wait_ge(zeroed, 10)
            dve.wait_ge(params_in, 16 * DEPTH * (3 + 2 * NF))

            def shifted_input(b):
                nc.vector.tensor_copy(xs[:], stream[:, batch(b, 0, PAD + T)]).then_inc(xs_done, 1)

            def step(it, u, tail=False):
                n = it * UNITS + u
                first = isinstance(it, int) and it == 0
                with_b = not (first and u < 1) and not (tail and u > 0)
                with_c = not (first and u < 2) and not (tail and u > 1)
                with_d = not (first and u < 3)
                if with_c:
                    dve.wait_ge(s_done, n - 1)
                    nc.vector.tensor_reduce(mx[:], SB_.rearrange("p (h k) -> p h k", k=2 * WIN), AX.X,
                                            ALU.max).then_inc(max_done, 1)
                    dve.wait_ge(max_done, n - 1)
                    need(dve, exp_done, n - 2)
                    nc.vector.tensor_tensor(sm[:], SB_.rearrange("p (h k) -> p h k", k=2 * WIN),
                                            mx[:].unsqueeze(2).broadcast_to([P, HH, 2 * WIN]),
                                            ALU.subtract).then_inc(sub_done, 1)
                if with_b:
                    dve.wait_ge(norm_qk, n)
                    need(dve, tab_done, (it + 1) if u else it)
                    nc.vector.tensor_tensor(qkc.rearrange("p (a h) d -> p a h d", a=2),
                                            qkn.rearrange("p (a h) d -> p a h d", a=2),
                                            tab[:, 2 * ((u - 1) % UNITS // 2), :].rearrange("p (a o d) -> p a o d", a=2, o=1)
                                            .broadcast_to([P, 2, HH, D]),
                                            ALU.mult).then_inc(cos_done, 1)
                    dve.wait_ge(cos_done, n)
                    dve.wait_ge(sin_done, n)
                    need(dve, qt_done, n - 1)
                    nc.vector.tensor_tensor(qkr[:].rearrange("p h (t f) -> p h t f", t=2),
                                            qkc.rearrange("p h (t f) -> p h t f", t=2),
                                            qks_.rearrange("p h (t f) -> p h t f", t=2)[:, :, ::-1, :],
                                            ALU.add).then_inc(rot_done, 1)
                if not tail:
                    dve.wait_ge(sq_done, n + 1)
                    nc.vector.tensor_reduce(ss[:], sq, AX.X, ALU.add).then_inc(red_done, 1)
                    dve.wait_ge(red_done, n + 1)
                    need(dve, rn_done, n)
                    nc.vector.tensor_scalar(cl[:], ss[:], 1e-24, None, ALU.max).then_inc(clamp_done, 1)
                if with_c:
                    dve.wait_ge(exp_done, n - 1)
                    nc.vector.tensor_reduce(lsum[:], pr[:, u % 2], AX.X, ALU.add).then_inc(sum_done, 1)
                    dve.wait_ge(sum_done, n - 1)
                    if u == UNITS - 1:
                        dve.wait_ge(v_done, n + 1)
                    nc.vector.reciprocal(rl[:], lsum[:]).then_inc(rl_done, 1)
                if not tail:
                    if u == UNITS - 1:
                        plain(dve)
                        shifted_input((it + 1) % B)
                    if not first:
                        ff(it, u, 0)
                        ff(it, u, 1)
                if with_c:
                    dve.wait_ge(rl_done, n - 1)
                    dve.wait_ge(pv_done, n - 1)
                    need(dve, ot_done, n - 2)
                    nc.vector.tensor_tensor(on[:], OB.rearrange("p (h d) -> p h d", d=D),
                                            rl[:].unsqueeze(2).broadcast_to([P, HH, D]), ALU.mult).then_inc(o_done, 1)
                if u < 2 and not tail:
                    for r in range(2):
                        last = nc.vector.memset(vwin[64 * r:64 * r + WIN, u, 0, :], 0.0)
                    last.then_inc(edge_zeroed, 1)
                if not tail:
                    dve.wait_ge(rn_done, n + 1)
                    dve.wait_ge(proj_done, n + 1)
                    need(dve, sin_done, n)
                    need(dve, cos_done, n)
                    nc.vector.tensor_tensor(qkn, QK.rearrange("p a (h d) -> p (a h) d", d=D),
                                            rn[:].unsqueeze(2).broadcast_to([P, 2 * HH, D]), ALU.mult).then_inc(norm_qk, 1)
                if with_d:
                    bb = (it if u >= 3 else it - 1) % B
                    at = PAD + (u - 3) % UNITS // 2 * P
                    dve.wait_ge(y_done, n - 2)
                    lo, hi = stream[0:64, batch(bb, at, P)], stream[64:128, batch(bb, at + 1, P)]
                    nc.vector.tensor_tensor(lo, TR[0:64, 0:P], lo, ALU.add).then_inc(y_added, 1)
                    nc.vector.tensor_tensor(hi, TR[64:128, 0:P], hi, ALU.add).then_inc(y_added, 1)
                if not first and not tail:
                    ff(it, u, 2)

            def ff(it, u, spot):
                bb, l = (it - 1) % B, (it - 1) // B
                if (u, spot) == (3, 0):
                    dve.wait_ge(mean_done, it)
                    dve.wait_ge(y_added, it * (2 * UNITS))
                    nc.vector.tensor_tensor(fd[:], stream[:, batch(bb, PAD, T)], FB, ALU.subtract).then_inc(dev_done, 1)
                if (u, spot) == (3, 2):
                    dve.wait_ge(var_done, it)
                    nc.vector.tensor_scalar(fv[:], FB[:, 0:NT], EPS, None, ALU.add).then_inc(fv_done, 1)
                if (u, spot) == (4, 0):
                    dve.wait_ge(frs_done, it)
                    nc.vector.tensor_tensor(fdg[:], ident[:].unsqueeze(1).broadcast_to([P, NT, P]),
                                            frs[:].unsqueeze(2).broadcast_to([P, NT, P]), ALU.mult).then_inc(dg_done, 1)
                if (u, spot) == (4, 2):
                    dve.wait_ge(bc_done, it)
                    nc.vector.tensor_tensor(fxn[:], fd[:], FB, ALU.mult).then_inc(xn_done, 1)
                if u == 6:
                    c = spot
                    m = FCH[c]
                    dve.wait_ge(up_done, (it - 1) * NF + c + 1)
                    dve.wait_ge(gelu_done, (it - 1) * NF + c + 1)
                    nc.vector.scalar_tensor_tensor(out=fh[0:m, c, :], in0=FB[0:m, :], scalar=b1a[0:m, c, bass.ds(l, 1)],
                                                   in1=fg[0:m, c, :], op0=ALU.add, op1=ALU.mult).then_inc(h_done, 1)
                if (u, spot) == (7, 0):
                    dve.wait_ge(down_done, it)
                    lo, hi = stream[0:64, batch(bb, PAD, T)], stream[64:128, batch(bb, PAD + 1, T)]
                    nc.vector.scalar_tensor_tensor(out=lo, in0=FB[0:64, :], scalar=b2[0:64, bass.ds(l, 1)], in1=lo,
                                                   op0=ALU.add, op1=ALU.add).then_inc(ff_added, 1)
                    nc.vector.scalar_tensor_tensor(out=hi, in0=FB[64:128, :], scalar=b2[64:128, bass.ds(l, 1)], in1=hi,
                                                   op0=ALU.add, op1=ALU.add).then_inc(ff_added, 1)

            shifted_input(0)
            for u in range(UNITS):
                step(0, u)
            with dve.Fori(1, ITERS) as it:
                for u in range(UNITS):
                    step(it, u)
            for u in range(3):
                step(ITERS, u, tail=True)
            for u in range(3, UNITS):
                for spot in range(3):
                    ff(ITERS, u, spot)
            def finish(pair, e):
                b, y = pair * 2 + e, ys[e]
                dve.wait_ge(back_done, b + 1)
                need(dve, stored[e], pair * 16)
                nc.vector.tensor_tensor(y[:], turned[e].rearrange("p (t c) -> p t c", c=C), x1[:, bass.ds(b * NT, NT), :],
                                        ALU.add).then_inc(fin_sum, 1)
                dve.wait_ge(fin_sum, b + 1)
                for t in range(NT):
                    last = nc.vector.bn_stats(bn[:, t, :], y[:, t, :])
                last.then_inc(fin_stats, 1)
                plain(dve)
                dve.wait_ge(fin_stats, b + 1)
                for t in range(NT):
                    last = nc.vector.bn_aggr(mv[:, t, :], bn[:, t, :])
                last.then_inc(fin_aggr, 1)
                dve.wait_ge(fin_aggr, b + 1)
                nc.vector.tensor_scalar(vv1[:], mv[:, :, 1], EPS, None, ALU.add).then_inc(fin_var, 1)
                dve.wait_ge(fin_rs, b + 1)
                for t in range(NT):
                    last = nc.vector.tensor_scalar(y[:, t, :], y[:, t, :], mv[:, t, 0:1], rs1[:, t:t + 1],
                                                   ALU.subtract, ALU.mult)
                last.then_inc(fin_done, 1)

            for e in range(2):
                finish(0, e)
            with dve.Fori(1, B // 2) as pair:
                for e in range(2):
                    finish(pair, e)

        @block.tensor
        def _(pe):
            def turn(dst, src):
                return nc.tensor.transpose(dst, src, ident[:])

            pe.wait_ge(consts_in, 16 * N_CONST)
            pe.wait_ge(w1nat_in, 48)
            for i in range(3):
                last = turn(FB[:, i * C:(i + 1) * C], w1nat[:, i, :])
            last.then_inc(wt_done, 1)
            pe.wait_ge(wt_copied, 7)
            pe.wait_ge(bf_ready, 3)
            def turn_input(nb):
                pe.wait_ge(xin_in, nb * 16 + 16)
                need(pe, mx1_done, nb * (G1 * MAXES))
                for t in range(NT):
                    last = turn(banks[:, 0, t * P:(t + 1) * P], xin[:, t, :])
                last.then_inc(xt1_done, 1)

            def project(nb, m):
                i, g = m % 2, m // 2
                if m == 0:
                    pe.wait_ge(xt1_copied, nb + 1)
                if m >= 4:
                    pe.wait_ge(lo1_done, nb * (2 * G1) + m - 3)
                w = (wq1, wk1)[i]
                nc.tensor.matmul(banks[:, m % 4, :], w[:, g * (P // SLOT):(g + 1) * (P // SLOT), :].rearrange("p h s -> p (h s)"),
                                 x1t[:], start=True, stop=True).then_inc(pj1_done, 1)

            def project_values(nb):
                need(pe, part1_done, nb * G1 - 1)
                for t in range(NT):
                    last = nc.tensor.matmul(FB[:, t * C:(t + 1) * C], x1t[:, t * P:(t + 1) * P], wv1[:], start=True, stop=True)
                last.then_inc(v1_done, 1)

            def scores(b, g, x):
                i, half = x // 2, x % 2
                if x == 0:
                    pe.wait_ge(kz_done, b * G1 + g + 1)
                    if g == 0:
                        pe.wait_ge(lo1_done, (b + 1) * (2 * G1))
                need(pe, mx1_done, b * (G1 * MAXES) + g * MAXES + x - 1)
                for r in range(2 * half, 2 * half + 2):
                    nc.tensor.matmul(banks[:, r, 0:(i + 1) * P], qk1[:, 0, g, i * P:(i + 1) * P],
                                     kz[:, g, r, 0:(i + 1) * P], start=True, stop=False)
                    last = nc.tensor.matmul(banks[:, r, i * P:(i + 1) * P], identb[:], maskb[:, 4 * WIN:4 * WIN + P],
                                            start=False, stop=True)
                last.then_inc(s1_done, 1)

            def turn_maxima(b, g):
                if g == 0:
                    pe.wait_ge(v1_copied, b + 1)
                    need(pe, part1_done, b * G1)
                elif g == 1:
                    need(pe, stream_in, 2 * b)
                else:
                    pe.wait_ge(part1_done, b * G1 + g - 1)
                pe.wait_ge(neg1_done, b * G1 + g + 1)
                for i in range(NT):
                    last = nc.tensor.transpose(FB.bitcast(F16)[:, i * P:(i + 1) * P],
                                               mnat[:, i, g * GH:(g + 1) * GH, :].rearrange("p r s -> p (r s)"), identh[:])
                last.then_inc(mt1_done, 1)

            def shifted(b, q, r):
                g, k = q // NT, q % NT
                e = (b * QUADS + q) * GH + r
                need(pe, exp1_done, e - 1)
                if k == 0:
                    pe.wait_ge(qm1_done, b * G1 + g + 1)
                nc.tensor.matmul(banks[:, 4 + r % 2, 0:T - k * P], kz[:, g, r, k * P:(k + 1) * P],
                                 qm1[:, g % 2, k * P:T], start=True, stop=False)
                nc.tensor.matmul(banks[:, 4 + r % 2, 0:P], identb[:], maskb[:, 4 * WIN + P:4 * WIN + 2 * P],
                                 start=False, stop=True).then_inc(st1_done, 1)

            def results1(b, q):
                g, k = q // NT, q % NT
                n = b * QUADS + q
                pe.wait_ge(exp1_done, n * GH + GH)
                if k == 0:
                    need(pe, ot1_copied, b * G1 + g)
                if q == 0:
                    pe.wait_ge(v1_copied, b + 1)
                for r in range(GH):
                    last = nc.tensor.matmul(banks[SLOT * r:SLOT * r + SLOT, 6, k * P:T], v1[:, k, g * GH + r, :],
                                            p1[:, q % 2, r, 0:T - k * P], start=(k == 0), stop=(k == NT - 1),
                                            tile_position=(0, SLOT * r), skip_group_check=True)
                last.then_inc(pv1_done, 1)

            def turn_results(b, g, more):
                pe.wait_ge(ot1_copied, b * G1 + g + 1)
                if g + 1 < G1:
                    pe.wait_ge(qm1_done, b * G1 + g + 2)
                elif more:
                    pe.wait_ge(v1_copied, b + 2)
                else:
                    pe.wait_ge(part1_done, b * G1 + g)
                for i in range(NT):
                    last = turn(FB[:, i * P:(i + 1) * P], ot1[:, i * P:(i + 1) * P])
                last.then_inc(on1_done, 1)

            def turn_normed(b):
                pe.wait_ge(ln1_chain, b * 5 + 4)
                pe.wait_ge(part1_done, b * G1 + G1)
                for t in range(NT):
                    last = turn(FB[:, t * P:(t + 1) * P], y1[:, t, :])
                last.then_inc(back1_done, 1)

            def attend(b, more):
                for q in range(QUADS):
                    g, k = q // NT, q % NT
                    ahead = more and g == G1 - 1
                    if g + 1 < G1:
                        scores(b, g + 1, 2 * k)
                    if ahead and k == 0:
                        turn_input(b + 1)
                    if ahead:
                        for m in AHEAD[k][0]:
                            project(b + 1, m)
                    shifted(b, q, 0)
                    shifted(b, q, 1)
                    if q:
                        results1(b, q - 1)
                    if g + 1 < G1:
                        scores(b, g + 1, 2 * k + 1)
                    if ahead:
                        for m in AHEAD[k][1]:
                            project(b + 1, m)
                    shifted(b, q, 2)
                    shifted(b, q, 3)
                    if g and k == 1:
                        turn_results(b, g - 1, more)
                    if q == 2 and not (isinstance(b, int) and b == 0):
                        turn_normed(b - 1)
                    if g + 1 < G1 and k == NT - 1:
                        turn_maxima(b, g + 1)
                if more:
                    project_values(b + 1)
                results1(b, QUADS - 1)
                if more:
                    for x in range(MAXES):
                        scores(b + 1, 0, x)
                        if x == 3:
                            turn_results(b, G1 - 1, more)
                    turn_maxima(b + 1, 0)
                else:
                    turn_results(b, G1 - 1, more)

            turn_input(0)
            for m in range(2 * G1):
                project(0, m)
            project_values(0)
            for x in range(MAXES):
                scores(0, 0, x)
            turn_maxima(0, 0)
            attend(0, True)
            with pe.Fori(1, B - 1) as b:
                attend(b, True)
            attend(B - 1, False)
            turn_normed(B - 1)

            pe.wait_ge(stream_in, 2 * B)

            def step(it, u, tail=False):
                n = it * UNITS + u
                first = isinstance(it, int) and it == 0
                j, hf = u // 2, u % 2
                pj, ph = (u - 1) % UNITS // 2, (u - 1) % 2
                with_b = not (first and u < 1) and not (tail and u > 0)
                with_c = not (first and u < 2) and not (tail and u > 1)
                with_d = not (first and u < 3)
                wv = wqkv[:, 2 * INNER + hf * 512:2 * INNER + (hf + 1) * 512].rearrange("p (h r d) -> p r h d", r=2, d=D)

                def values():
                    need(pe, v_copied, n)
                    for w in range(NW):
                        for r in range(2):
                            at = 64 * r + (WIN if w % 2 == 0 else 0)
                            last = nc.tensor.matmul(VB[at:at + WIN, (w // 2) * 256:(w // 2 + 1) * 256].rearrange("p (h d) -> p h d", d=D),
                                                    xs[:, PAD + j * P + w * WIN:PAD + j * P + (w + 1) * WIN], wv[:, r],
                                                    start=True, stop=True, tile_position=(0, at))
                    last.then_inc(v_done, 1)

                def scores(par):
                    r = 64 * par
                    for h in range(par, HH, 2):
                        for w in range(NW):
                            at = pj * P + w * WIN
                            last = nc.tensor.matmul(SB_[32 * w:32 * w + 32, h * 2 * WIN:(h + 1) * 2 * WIN],
                                                    qT[r:r + 64, h // 2, 32 * w:32 * w + 32],
                                                    kT[r:r + 64, ph * HP + h // 2, at:at + 2 * WIN],
                                                    start=False, stop=True, tile_position=(r, 32 * w),
                                                    skip_group_check=True)
                    return last

                def results(par):
                    r = 64 * par
                    for h in range(par, HH, 2):
                        for w in range(NW):
                            last = nc.tensor.matmul(OB[32 * w:32 * w + 32, h * D:(h + 1) * D],
                                                    pT[r:r + 64, h // 2, 32 * w:32 * w + 32],
                                                    vwin[r:r + 64, (u - 2) % 4, w, h // 2 * D:(h // 2 + 1) * D],
                                                    start=True, stop=True, tile_position=(r, 32 * w))
                    return last

                if with_d:
                    pe.wait_ge(o_done, n - 2)
                    need(pe, pt_copied, n - 2)
                    for h in range(HP):
                        last = turn(PO[:, h * P:(h + 1) * P], on[:, 2 * h:2 * h + 2, :].rearrange("p h d -> p (h d)"))
                    last.then_inc(ot_done, 1)
                if not tail:
                    if u == 0:
                        pe.wait_ge(wqkv_in, (it // B) * 16 + 16)
                        pe.wait_ge(xs_done, it + 1)
                    need(pe, norm_qk, n)
                    need(pe, sq_done, n)
                    for i in range(2):
                        last = nc.tensor.matmul(QK[:, i, :], xs[:, PAD + j * P:PAD + (j + 1) * P],
                                                wqkv[:, i * INNER + hf * 512:i * INNER + hf * 512 + 512], start=True, stop=True)
                    last.then_inc(proj_done, 1)
                    values()
                    if not first:
                        ff(it, u, 0)
                if with_c:
                    if u in (2, 3):
                        pe.wait_ge(edge_zeroed, it * 2 + u - 1)
                    pe.wait_ge(exp_done, n - 1)
                    need(pe, ot_copied, n - 2)
                    for h in range(HP):
                        last = turn(PO[:, h * P:(h + 1) * P], pr[:, u % 2, 2 * h:2 * h + 2, :].rearrange("p h d -> p (h d)"))
                    last.then_inc(pt_done, 1)
                if with_b:
                    need(pe, sub_done, n - 1)
                    m = maskb[:, 0:2 * WIN] if pj else maskb[:, 2 * WIN:4 * WIN]
                    nc.tensor.matmul(SB_.rearrange("p (h k) -> p h k", k=2 * WIN), identb[:],
                                     m.unsqueeze(1).broadcast_to([P, HH, 2 * WIN]), start=True, stop=False,
                                     skip_group_check=True)
                    pe.wait_ge(rot_done, n)
                    need(pe, qt_copied, n - 1)
                    need(pe, y_added, 2 * (n - 3))
                    for h in range(HP):
                        last = turn(TR[:, h * P:(h + 1) * P], qkr[:, HH + 2 * h:HH + 2 * h + 2, :].rearrange("p h d -> p (h d)"))
                    last.then_inc(kt_done, 1)
                if with_c:
                    if tail and u == 1:
                        pe.wait_ge(v_copied, ITERS * UNITS)
                    plain(pe)
                    pe.wait_ge(pt_copied, n - 1)
                    need(pe, o_done, n - 2)
                    results(1).then_inc(pv_odd, 1)
                if with_b:
                    pe.wait_ge(kt_copied, n)
                    for h in range(HP):
                        last = turn(TR[:, h * P:(h + 1) * P], qkr[:, 2 * h:2 * h + 2, :].rearrange("p h d -> p (h d)"))
                    last.then_inc(qt_done, 1)
                if with_c:
                    plain(pe)
                    pe.wait_ge(pv_odd, n - 1)
                    results(0).then_inc(pv_done, 1)
                if not first and not tail:
                    ff(it, u, 1)
                if with_b:
                    plain(pe)
                    pe.wait_ge(qt_copied, n)
                    scores(0).then_inc(s_even, 1)
                if with_d:
                    if u == 3:
                        pe.wait_ge(wo_in, (it // B) * 16 + 16)
                    pe.wait_ge(ot_copied, n - 2)
                    pe.wait_ge(qt_copied, min(n, ITERS * UNITS) if tail else n)
                    if tail:
                        pe.wait_ge(y_added, 2 * (n - 3))
                    for h in range(HP):
                        last = nc.tensor.matmul(TR[:, 0:P], wo[:, (u - 3) % 2 * HP + h, :], oT[:, (u - 3) % 2, h, :],
                                                start=(h == 0), stop=(h == HP - 1))
                    last.then_inc(y_done, 1)
                if with_b:
                    plain(pe)
                    pe.wait_ge(s_even, n)
                    scores(1).then_inc(s_done, 1)
                if not first and not tail:
                    ff(it, u, 2)

            def ff(it, u, spot):
                bb, l = (it - 1) % B, (it - 1) // B
                if (u, spot) == (3, 0):
                    pe.wait_ge(y_added, it * (2 * UNITS))
                    nc.tensor.matmul(FB, mean_w[:], stream[:, batch(bb, PAD, T)], start=True, stop=True).then_inc(mean_done, 1)
                if (u, spot) == (3, 2):
                    pe.wait_ge(fsq_done, it)
                    for t in range(NT):
                        last = nc.tensor.matmul(FB[:, t:t + 1], fsq[:, t * P:(t + 1) * P], mean_w[:, 0:1], start=True, stop=True)
                    last.then_inc(var_done, 1)
                if (u, spot) == (4, 1):
                    pe.wait_ge(dg_done, it)
                    nc.tensor.matmul(FB, ones[:], fdg[:].rearrange("p t c -> p (t c)"), start=True, stop=True).then_inc(bc_done, 1)
                if u == 5:
                    c = spot
                    m = FCH[c]
                    if c == 0:
                        pe.wait_ge(w1_in, l * 16 + 16)
                        pe.wait_ge(xa_done, it)
                    else:
                        pe.wait_ge(gelu_done, (it - 1) * NF + c)
                    nc.tensor.matmul(FB[0:m, :], w1[:, FF + c * P:FF + c * P + m], fxa[:], start=True, stop=True).then_inc(gate_done, 1)
                if u == 6:
                    c = spot
                    m = FCH[c]
                    if c == 0:
                        pe.wait_ge(gelu_done, it * NF)
                    else:
                        pe.wait_ge(h_done, (it - 1) * NF + c)
                    nc.tensor.matmul(FB[0:m, :], w1[:, c * P:c * P + m], fxa[:], start=True, stop=True).then_inc(up_done, 1)
                if (u, spot) == (7, 0):
                    pe.wait_ge(h_done, it * NF)
                    pe.wait_ge(w2_in, l * (16 * NF) + 16 * NF)
                    for c in range(NF):
                        m = FCH[c]
                        last = nc.tensor.matmul(FB, w2[0:m, c, :], fh[0:m, c, :], start=(c == 0), stop=(c == NF - 1))
                    last.then_inc(down_done, 1)

            for u in range(UNITS):
                step(0, u)
            with pe.Fori(1, ITERS) as it:
                for u in range(UNITS):
                    step(it, u)
            for u in range(3):
                step(ITERS, u, tail=True)
            for u in range(3, UNITS):
                for spot in range(3):
                    ff(ITERS, u, spot)
            def finish(b, e):
                pe.wait_ge(flat_done, b * 2 + 2)
                need(pe, fin_sum, b - 1)
                for t in range(NT):
                    last = turn(turned[e][:, t * P:(t + 1) * P], flats[e][:, t * P:(t + 1) * P])
                last.then_inc(back_done, 1)

            finish(0, 0)
            finish(1, 1)
            with pe.Fori(1, B // 2) as pair:
                finish(pair * 2, 0)
                finish(pair * 2 + 1, 1)


_INS = ['L0_attn_x', 'L0_attn_Wq', 'L0_attn_Wk', 'L0_attn_Wv', 'L0_ffn_Wqkv', 'L0_ffn_q_scale', 'L0_ffn_k_scale',
        'L0_ffn_Wo', 'L0_ffn_ln_g', 'L0_ffn_ln_b', 'L0_ffn_W1', 'L0_ffn_b1', 'L0_ffn_W2', 'L0_ffn_b2']
_CONSTS = ['rot', 'masks', 'ident', 'parts']


def kernel(**inputs):
    import numpy as _np
    import concourse.bacc as _bacc
    from concourse import mybir as _mybir
    from concourse.bass_utils import run_bass_kernel_spmd as _run

    nc = _bacc.Bacc("TRN2", target_bir_lowering=False, num_devices=1)
    arrays, args = {}, []
    consts = constants()
    for name in _INS + _CONSTS:
        a = _np.ascontiguousarray(inputs[name] if name in _INS else consts[name])
        arrays[f"in_{name}_dram"] = a
        args.append(nc.dram_tensor(f"in_{name}_dram", a.shape, _mybir.dt.from_np(a.dtype), kind="ExternalInput").ap())
    args.append(nc.dram_tensor("out_0_dram", (B, T, C), _mybir.dt.float32, kind="ExternalOutput").ap())
    build(nc, *args)
    r = _run(nc, [arrays], core_ids=[0])
    return r.results[0]["out_0_dram"]
```
